# Optimizing a Trainium2 kernel written in Bass

```python
import numpy as np
import jax
import jax.numpy as jnp

def _softmax(x, axis=-1):
    return jax.nn.softmax(x, axis=axis)

def _gelu(x):
    return jax.nn.gelu(x, approximate=True)

def _silu(x):
    return jax.nn.silu(x)

def _sigmoid(x):
    return jax.nn.sigmoid(x)

def _layernorm(x, axis=-1, eps=1e-05):
    m = jnp.mean(x, axis=axis, keepdims=True)
    v = jnp.var(x, axis=axis, keepdims=True)
    return (x - m) / jnp.sqrt(v + eps)

def _scatter_add(tgt, idx, src, axis=0):
    return tgt.at[idx].add(src)

def _segment_sum(src, seg, n):
    return jax.ops.segment_sum(src, seg, n)
kernel_name = 'mk_adj_preln_d4_adj_r2_fed481'

def setup_inputs(seed: int=0):
    np.random.seed(seed)
    _w = jnp.asarray

    def _rec_inputs():
        import jax
        import jax.numpy as jnp
        _gk = jax.random.key(seed)
        x = -0.0005146 + 1 * jax.random.normal(jax.random.fold_in(_gk, 1), (8, 1024, 128), jnp.float32)
        _a = jax.random.bernoulli(jax.random.fold_in(_gk, 2), 0.00390625, (8, 1024, 1024))
        _a = jnp.logical_or(_a, jnp.swapaxes(_a, -1, -2))
        _a = jnp.logical_or(_a, jnp.eye(1024, dtype=bool))
        adj = _a.astype(jnp.int32)
        return (x, adj)
    x, adj = _rec_inputs()

    def _L0_gnn_setup():
        import jax, jax.numpy as jnp
        import numpy as np
        B, N, C, OUT, S = (4, 1024, 128, 128, 25)
        DENSITY = 0.008
        key = jax.random.key(seed)
        kA, kX, kW = jax.random.split(key, 3)
        A = jax.random.bernoulli(kA, DENSITY, (B, N, N)).astype(jnp.int32)
        X = jax.random.normal(kX, (B, N, C), dtype=jnp.float32)
        W = jax.random.normal(kW, (2 * C, OUT), dtype=jnp.float32) * np.float32(1.0 / np.sqrt(2 * C))
        b = jnp.zeros((OUT,), dtype=jnp.float32)
        return {'A': A, 'X': X, 'W': W, 'b': b}
    _L0_gnn_all = _L0_gnn_setup()
    _L0_gnn_in = {k: v for k, v in _L0_gnn_all.items() if k in ('W', 'b')}
    del _L0_gnn_all

    def _L1_gnn_setup():
        import jax, jax.numpy as jnp
        import numpy as np
        ALPHA = 0.2
        NEG_INF = -9000000000000000.0
        key = jax.random.key(seed)
        k_h, k_adj, k_W, k_a = jax.random.split(key, 4)
        B, N, Din, Dout = (8, 512, 128, 128)
        h = jax.random.normal(k_h, (B, N, Din), dtype=jnp.float32)
        adj = jax.random.randint(k_adj, (B, N, N), 0, 2, dtype=jnp.int32)
        W = jax.random.normal(k_W, (Dout, Din), dtype=jnp.float32) * (1.0 / np.sqrt(Din))
        lim = np.float32(1.414 * np.sqrt(6.0 / (2 * Dout + 1)))
        a = jax.random.uniform(k_a, (2 * Dout, 1), dtype=jnp.float32, minval=-lim, maxval=lim)
        return {'h': h, 'adj': adj, 'W': W, 'a': a}
    _L1_gnn_all = _L1_gnn_setup()
    _L1_gnn_in = {k: v for k, v in _L1_gnn_all.items() if k in ('W', 'a')}
    del _L1_gnn_all

    def _L2_gnn_setup():
        import jax, jax.numpy as jnp
        import numpy as np
        D = 128
        B, N = (16, 512)
        NEG_SLOPE = 0.2
        SCALE = float(np.sqrt(D))
        key = jax.random.key(seed)
        ks = jax.random.split(key, 8)
        s = 1.0 / np.sqrt(D)
        return {'feature': jax.random.normal(ks[0], (B, N, D), dtype=jnp.float32), 'graph': jax.random.randint(ks[1], (B, N, N), 0, 2, dtype=jnp.int32), 'W_w': jax.random.uniform(ks[2], (D, D), jnp.float32, -s, s), 'W_b': jax.random.uniform(ks[3], (D,), jnp.float32, -s, s), 'Q_w': jax.random.uniform(ks[4], (D, D), jnp.float32, -s, s), 'Q_b': jax.random.uniform(ks[5], (D,), jnp.float32, -s, s), 'K_w': jax.random.uniform(ks[6], (D, D), jnp.float32, -s, s), 'K_b': jax.random.uniform(ks[7], (D,), jnp.float32, -s, s)}
    _L2_gnn_all = _L2_gnn_setup()
    _L2_gnn_in = {k: v for k, v in _L2_gnn_all.items() if k in ('W_w', 'W_b', 'Q_w', 'Q_b', 'K_w', 'K_b')}
    del _L2_gnn_all

    def _L3_gnn_setup():
        import jax, jax.numpy as jnp
        import numpy as np
        B, N, D_IN, D_OUT, H = (8, 512, 128, 128, 8)
        HD = D_OUT // H
        ALPHA = 0.2
        key = jax.random.key(seed)
        k1, k2, k3, k4 = jax.random.split(key, 4)
        h = jax.random.normal(k1, (B, N, D_IN), dtype=jnp.float32)
        adj_mask = jax.random.randint(k2, (B, N, N), 0, 2, dtype=jnp.int64)
        idx = jnp.arange(N)
        adj_mask = adj_mask.at[:, idx, idx].set(1)
        lim_W = float(np.sqrt(6.0 / (D_IN + D_OUT)))
        W = jax.random.uniform(k3, (D_IN, D_OUT), minval=-lim_W, maxval=lim_W, dtype=jnp.float32)
        lim_a = float(np.sqrt(6.0 / (2 * HD + 1)))
        a = jax.random.uniform(k4, (2 * HD,), minval=-lim_a, maxval=lim_a, dtype=jnp.float32)
        return {'h': h, 'adj_mask': adj_mask, 'W': W, 'a': a}
    _L3_gnn_all = _L3_gnn_setup()
    _L3_gnn_in = {k: v for k, v in _L3_gnn_all.items() if k in ('W', 'a')}
    del _L3_gnn_all
    return {'x': x, 'adj': adj, 'L0_gnn_W': _L0_gnn_in['W'], 'L0_gnn_b': _L0_gnn_in['b'], 'L1_gnn_W': _L1_gnn_in['W'], 'L1_gnn_a': _L1_gnn_in['a'], 'L2_gnn_W_w': _L2_gnn_in['W_w'], 'L2_gnn_W_b': _L2_gnn_in['W_b'], 'L2_gnn_Q_w': _L2_gnn_in['Q_w'], 'L2_gnn_Q_b': _L2_gnn_in['Q_b'], 'L2_gnn_K_w': _L2_gnn_in['K_w'], 'L2_gnn_K_b': _L2_gnn_in['K_b'], 'L3_gnn_W': _L3_gnn_in['W'], 'L3_gnn_a': _L3_gnn_in['a']}

def reference(x, adj, L0_gnn_W, L0_gnn_b, L1_gnn_W, L1_gnn_a, L2_gnn_W_w, L2_gnn_W_b, L2_gnn_Q_w, L2_gnn_Q_b, L2_gnn_K_w, L2_gnn_K_b, L3_gnn_W, L3_gnn_a):
    import jax
    import jax.numpy as jnp

    def _L0_gnn_ref(A, X, W, b):
        import jax, jax.numpy as jnp
        import numpy as np
        B, N, C, OUT, S = (4, 1024, 128, 128, 25)
        DENSITY = 0.008
        mask = A != 0
        neg_inf = jnp.float32(-jnp.inf)
        pri = -jnp.arange(N, dtype=jnp.float32)
        scores = jnp.where(mask, pri, neg_inf)
        vals, idx = jax.lax.top_k(scores, S)
        valid = vals > neg_inf
        feats = jax.vmap(lambda x, i: x[i])(X, idx)
        feats = jnp.where(valid[..., None], feats, neg_inf)
        agg = feats.max(axis=2)
        degree = mask.sum(axis=-1)
        agg = jnp.where((degree <= S)[..., None], jnp.maximum(agg, 0.0), agg)
        h = jnp.concatenate([X, agg], axis=-1)
        out = jax.nn.relu(jnp.einsum('bnf,fo->bno', h, W) + b)
        return out

    def _L1_gnn_ref(h, adj, W, a):
        import jax, jax.numpy as jnp
        import numpy as np
        ALPHA = 0.2
        NEG_INF = -9000000000000000.0
        Wh = jnp.einsum('bnd,fd->bnf', h, W)
        F_ = Wh.shape[-1]
        a1 = a[:F_, 0]
        a2 = a[F_:, 0]
        src = Wh @ a1
        dst = Wh @ a2
        e = src[:, :, None] + dst[:, None, :]
        e = jnp.where(e > 0, e, ALPHA * e)
        e = jnp.where(adj > 0, e, NEG_INF)
        attention = jax.nn.softmax(e, axis=-1)
        h_prime = jnp.einsum('bij,bjf->bif', attention, Wh)
        return h_prime

    def _L2_gnn_ref(feature, graph, W_w, W_b, Q_w, Q_b, K_w, K_b):
        import jax, jax.numpy as jnp
        import numpy as np
        D = 128
        B, N = (16, 512)
        NEG_SLOPE = 0.2
        SCALE = float(np.sqrt(D))
        h = jnp.einsum('bnd,ed->bne', feature, W_w) + W_b
        q = jnp.einsum('bnd,ed->bne', h, Q_w) + Q_b
        k = jnp.einsum('bnd,ed->bne', h, K_w) + K_b
        e = jnp.einsum('bnd,bmd->bnm', q, k) / SCALE
        e = jnp.where(e >= 0, e, NEG_SLOPE * e)
        e = jnp.where(graph == 0, jnp.float32(-1000000000.0), e)
        a = jax.nn.softmax(e, axis=2)
        out = jax.nn.relu(jnp.einsum('bnm,bmd->bnd', a, h))
        return out

    def _L3_gnn_ref(h, adj_mask, W, a):
        import jax, jax.numpy as jnp
        import numpy as np
        B, N, D_IN, D_OUT, H = (8, 512, 128, 128, 8)
        HD = D_OUT // H
        ALPHA = 0.2
        b, n, _ = h.shape
        Wh = (h @ W).reshape(b, n, H, HD).transpose(0, 2, 1, 3)
        a1, a2 = (a[:HD], a[HD:])
        e1 = jnp.einsum('bhnd,d->bhn', Wh, a1)
        e2 = jnp.einsum('bhnd,d->bhn', Wh, a2)
        e = e1[:, :, :, None] + e2[:, :, None, :]
        mask = adj_mask[:, None, :, :] == 0
        e = jnp.where(mask, -jnp.inf, e)
        e = jnp.where(e >= 0, e, ALPHA * e)
        attn = jax.nn.softmax(e, axis=-1)
        h_prime = jnp.einsum('bhij,bhjd->bhid', attn, Wh)
        return h_prime.transpose(0, 2, 1, 3).reshape(b, n, D_OUT)
    h = jnp.maximum(_layernorm(x, axis=-1), 0.0)
    x = x + _L0_gnn_ref(adj, h, L0_gnn_W, L0_gnn_b)
    h = jnp.maximum(_layernorm(x, axis=-1), 0.0)
    x = x + _L1_gnn_ref(h, adj, L1_gnn_W, L1_gnn_a)
    h = jnp.maximum(_layernorm(x, axis=-1), 0.0)
    x = x + _L2_gnn_ref(h, adj, L2_gnn_W_w, L2_gnn_W_b, L2_gnn_Q_w, L2_gnn_Q_b, L2_gnn_K_w, L2_gnn_K_b)
    h = jnp.maximum(_layernorm(x, axis=-1), 0.0)
    x = x + _L3_gnn_ref(h, adj, L3_gnn_W, L3_gnn_a)
    return x

_drawn_inputs = setup_inputs


def setup_inputs(seed=0):
    import zlib

    import numpy as np

    out = dict(_drawn_inputs(seed))
    spreads = {'L0_gnn_b': (0.0, 0.1)}
    factors = {'L2_gnn_Q_w': 8.0, 'L2_gnn_Q_b': 8.0, 'L2_gnn_K_w': 8.0, 'L2_gnn_K_b': 200.0}
    for name, (base, spread) in spreads.items():
        noise = np.random.default_rng([zlib.crc32(name.encode()), seed]).standard_normal(out[name].shape)
        drawn = base * np.exp(spread * noise) if base else spread * noise
        out[name] = jnp.asarray(drawn.astype(out[name].dtype))
    for name, factor in factors.items():
        out[name] = (out[name] * factor).astype(out[name].dtype)
    return out
```

```python
import concourse.bass as bass
from concourse import mybir
from contextlib import ExitStack

F32 = mybir.dt.float32
BF16 = mybir.dt.bfloat16
I32 = mybir.dt.int32
U32 = mybir.dt.uint32
ALU = mybir.AluOpType
ACT = mybir.ActivationFunctionType
AX = mybir.AxisListType

P = 128
SLOTS = 25
TOP = 32
EPS = 1e-5
SLOPE = 0.2
MASKED = 1.0e9


class Own:

    def __init__(self):
        self.value = 0

    def one(self):
        self.value += 1
        return 1


def graph_layers_kernel(nc, x, adj, w0, b0, w1, w1_t, a1, ww_t, wb, qw_t, qb, kw_t, kb, w3, a3, out):
    B, N, C = x.shape
    T = N // P
    HALF = T // 2
    HEADS = 8
    HD = C // HEADS
    GAT = [(1, C), (HEADS, HD)]
    SCORE_SCALE = 1.0 / float(C) ** 0.5
    RING = 2

    x_d = x.rearrange("b (t p) c -> b p t c", p=P)
    adj_d = adj.rearrange("b (t p) j -> b p t j", p=P)
    out_d = out.rearrange("b (t p) c -> b p t c", p=P)
    table = nc.dram_tensor("feature_table", [N + 1, C], F32, kind="Internal").ap()
    table_rows = table[0:N, :].rearrange("(t p) c -> p t c", p=P)

    with ExitStack() as ctx:
        def sb(name, shape, dt=F32):
            return ctx.enter_context(nc.sbuf_tensor(name, shape, dt))

        def ps(name, shape, dt=F32):
            return ctx.enter_context(nc.psum_tensor(name, shape, dt))

        def sem(name):
            return ctx.enter_context(nc.semaphore(name))

        w0_sb = sb("w0_sb", [P, 2, C])
        b0_sb = sb("b0_sb", [1, C])
        w1_sb = sb("w1_sb", [P, C])
        a1_sb = sb("a1_sb", [P, 2])
        wcat = [sb("wcat1", [P, C + 2]), sb("wcat3", [P, C + 2 * HEADS])]
        src_bc = sb("src_bc", [P, 1 + HEADS, P])
        ww_sb = sb("ww_sb", [P, C])
        qw_sb = sb("qw_sb", [P, C])
        kw_sb = sb("kw_sb", [P, C])
        wb_row = sb("wb_row", [1, C])
        cols = sb("cols", [P, 4])
        a3_sb = sb("a3_sb", [P, 2 * HD])
        a3_prod = sb("a3_prod", [P, HEADS, HD])
        ident = sb("ident", [P, P])
        identb = sb("identb", [P, P], BF16)
        ident_big = sb("ident_big", [P, P], BF16)
        ones = sb("ones", [P, P])
        eps_sb = sb("eps_sb", [P, 1])
        pri_i = sb("pri_i", [P, N], I32)
        zero_row = sb("zero_row", [1, C])

        adj_sb = sb("adj_sb", [P, T, N], I32)
        xin = sb("xin", [P, T, C])
        h0 = sb("h0", [P, T, C])
        h0_t = sb("h0_t", [P, N])
        agg = h0
        score = sb("score", [P, N])
        vals = sb("vals", [P, T, TOP])
        idx = sb("idx", [P, T, TOP], U32)
        gathered = sb("gathered", [P, RING, SLOTS * C])
        n_st = sb("n_st", [P, T, 6])
        n_mv = sb("n_mv", [P, T, 2])
        n_rstd = sb("n_rstd", [P, T])
        n_shift = sb("n_shift", [P, T])

        xres = sb("xres", [P, T, C])
        outb = sb("outb", [P, T, C])
        h = sb("h", [P, T, C])
        h_t = sb("h_t", [P, N])
        agg_t = h_t
        st = sb("st", [P, T, 6])
        mv = sb("mv", [P, T, 2])
        rstd = sb("rstd", [P, T])
        shift = sb("shift", [P, T])
        nmask = sb("nmask", [P, T, N], BF16)
        mask_t = sb("mask_t", [P, T, N], BF16)
        pos = sb("pos", [P, 2, T, N], BF16)
        v_words = T * HEADS * 2 * (HD + 1)
        v_sb = sb("v_sb", [P, v_words])
        vp_sb = sb("vp_sb", [P, 3 * v_words], BF16)
        v = [v_sb[:, 0:T * 2 * (C + 1)].rearrange("p (t h w) -> p t h w", t=T, h=1),
             v_sb[:, :].rearrange("p (t h w) -> p t h w", t=T, h=HEADS)]
        vp = [vp_sb[:, 0:T * 6 * (C + 1)].rearrange("p (t h k w) -> p t h k w", t=T, h=1, k=3),
              vp_sb[:, :].rearrange("p (t h k w) -> p t h k w", t=T, h=HEADS, k=3)]
        dmax = sb("dmax", [HEADS, 1])
        dmax_diag = sb("dmax_diag", [HEADS, HEADS])
        dmax_all = sb("dmax_all", [P, HEADS])
        dist = sb("dist", [P, T, HEADS])
        neg_dst = sb("neg_dst", [P, T, HEADS])
        reach = sb("reach", [P, T, HEADS])
        beta = sb("beta", [P, T, HEADS])
        o1 = sb("o1", [P, 2, 3 * (C + 1)])
        o1_tot = sb("o1_tot", [P, 2, C + 1])
        recip = sb("recip", [P, T, HEADS])
        head_out = v_sb[:, :].rearrange("p (h t w) -> p h t w", h=HEADS, t=T)
        all_out = sb("all_out", [P, T, HEADS, HD + 1])
        pos_f = pos[:, :, :, :].rearrange("p a t n -> p (a t n)").bitcast(F32)
        e_relu = [pos_f[:, i * N:(i + 1) * N] for i in (0, 1)]
        e_sb = [pos_f[:, i * N:(i + 1) * N] for i in (2, 3)]
        p_t = [pos_f[:, i * N:(i + 1) * N] for i in (4, 5)]
        hp_t = pos_f[:, 6 * N:7 * N]
        hp = pos_f[:, 7 * N:8 * N].rearrange("p (t c) -> p t c", t=T)
        q_t = v_sb[:, 0:N]
        k_t = v_sb[:, N:2 * N]
        row_max = sb("row_max", [P, T])
        neg_max = sb("neg_max", [P, T])
        row_sum = sb("row_sum", [P, T])
        o2 = sb("o2", [P, 2, C])

        ps_e = ps("ps_e", [P, 4, 512])
        ps_a = ps("ps_a", [P, 2, 512])
        ps_m = ps("ps_m", [P, 512])
        ps_n = ps("ps_n", [P, 512])
        slots_e = ps_e[:, :, :].rearrange("p b (s w) -> p (b s) w", s=2)
        wide_e = [ps_e[:, 2 * i:2 * i + 2, :].rearrange("p b w -> p (b w)") for i in (0, 1)]
        wide_a = ps_a[:, :, :].rearrange("p b w -> p (b w)")
        tiles_a = wide_a.rearrange("p (t w) -> p t w", t=T)
        mask_ps = [ps_e[:, i, :].bitcast(BF16) for i in range(4)]

        GATHER_SIGNALS = 16 * SLOTS * T // RING
        weights_in = sem("weights_in")
        consts = sem("consts")
        setup_v = sem("setup_v")
        setup_pe = sem("setup_pe")
        zero_stored = sem("zero_stored")
        x_loaded = sem("x_loaded")
        adj_loaded = [sem(f"adj_loaded{q}") for q in range(4)]
        table_stored = sem("table_stored")
        n_moments = sem("n_moments")
        n_rstd_ready = sem("n_rstd_ready")
        n_shift_ready = sem("n_shift_ready")
        h0_ready = sem("h0_ready")
        h0_turned = sem("h0_turned")
        h0_t_ready = sem("h0_t_ready")
        idx_ready = sem("idx_ready")
        gather_done = [sem(f"gather_done{r}") for r in range(RING)]
        gathers_begun = sem("gathers_begun")
        agg_ready = sem("agg_ready")
        agg_turned = sem("agg_turned")
        agg_t_ready = sem("agg_t_ready")
        linear_done = sem("linear_done")
        x1_ready = sem("x1_ready")
        v_next = sem("v_next")

        nmask_ready = sem("nmask_ready")
        mask_turned = sem("mask_turned")
        mask_t_ready = sem("mask_t_ready")
        moments = sem("moments")
        act_own = sem("act_own")
        rstd_ready = sem("rstd_ready")
        shift_ready = sem("shift_ready")
        h_ready = sem("h_ready")
        h_turned = sem("h_turned")
        h_t_ready = sem("h_t_ready")
        wh_done = sem("wh_done")
        dst_done = sem("dst_done")
        diag_ready = sem("diag_ready")
        dmax_spread = sem("dmax_spread")
        dist_ready = sem("dist_ready")
        exps_ready = sem("exps_ready")
        v_ready = sem("v_ready")
        part_ready = sem("part_ready")
        rest_ready = sem("rest_ready")
        parts_done = sem("parts_done")
        src_spread = sem("src_spread")
        pos_ready = sem("pos_ready")
        out1_done = sem("out1_done")
        o1_ready = sem("o1_ready")
        x2_ready = sem("x2_ready")
        hp_t_done = sem("hp_t_done")
        hp_t_ready = sem("hp_t_ready")
        qk_done = sem("qk_done")
        qk_ready = sem("qk_ready")
        hp_done = sem("hp_done")
        hp_ready = sem("hp_ready")
        scores_done = sem("scores_done")
        relu_ready = sem("relu_ready")
        masking_begun = sem("masking_begun")
        masked_ready = sem("masked_ready")
        neg_max_ready = sem("neg_max_ready")
        probs_ready = sem("probs_ready")
        probs_turned = sem("probs_turned")
        probs_t_ready = sem("probs_t_ready")
        out2_done = sem("out2_done")
        x3_ready = sem("x3_ready")
        all_done = sem("all_done")
        all_ready = sem("all_ready")
        head_done = sem("head_done")
        head_ready = sem("head_ready")
        x4_ready = sem("x4_ready")
        stored = sem("stored")
        v_att = sem("v_att")

        block = ctx.enter_context(nc.Block())

        @block.sync
        def _(sp):
            loads = [(w0_sb[:, :, :], w0.rearrange("(k p) o -> p k o", p=P)),
                     (b0_sb[:, :], b0.rearrange("(a n) -> a n", a=1)),
                     (w1_sb[:, :], w1), (wcat[0][:, 0:C], w1_t),
                     (a1_sb[:, :], a1),
                     (ww_sb[:, :], ww_t), (qw_sb[:, :], qw_t), (kw_sb[:, :], kw_t),
                     (wb_row[:, :], wb.rearrange("(a n) -> a n", a=1)),
                     (cols[:, 0:1], wb.rearrange("(p a) -> p a", a=1)),
                     (cols[:, 1:2], qb.rearrange("(p a) -> p a", a=1)),
                     (cols[:, 2:3], kb.rearrange("(p a) -> p a", a=1)),
                     (wcat[1][:, 0:C], w3), (a3_sb[:, :], a3)]

            def load_next(b, nb):
                if b is not None:
                    sp.wait_ge(x1_ready, b * 2 + 2)
                sp.dma_start(xin[:, :, :], x_d[nb]).then_inc(x_loaded, 16)
                for q in range(4):
                    if b is not None:
                        sp.wait_ge(nmask_ready, b * T + 2 * q + 2)
                    sp.dma_start(adj_sb[:, 2 * q:2 * q + 2, :], adj_d[nb, :, 2 * q:2 * q + 2, :])\
                        .then_inc(adj_loaded[q], 16)

            def store_table(nb, first):
                sp.wait_ge(h0_ready, nb * T + T)
                if not first:
                    sp.wait_ge(agg_ready, nb * T)
                sp.dma_start(table_rows, h0[:, :, :]).then_inc(table_stored, 16)

            def store_out(b):
                sp.wait_ge(x4_ready, b + 1)
                sp.dma_start(out_d[b], outb[:, :, :]).then_inc(stored, 16)

            load_next(None, 0)
            for dst, src in loads:
                sp.dma_start(dst, src).then_inc(weights_in, 16)
            sp.wait_ge(consts, 1)
            sp.dma_start(table[N:N + 1, :], zero_row[:, :]).then_inc(zero_stored, 16)
            store_table(0, True)
            with sp.Fori(0, B - 1) as b:
                load_next(b, b + 1)
                store_table(b + 1, False)
                store_out(b)
            store_out(B - 1)
            sp.wait_ge(stored, B * 16)

        N_WEIGHTS = 14 * 16

        @block.gpsimd
        def _(pool):
            pool.memset(zero_row[:, :], 0.0).then_inc(consts, 1)
            pool.memset(ident[:, :], 0.0).then_inc(consts, 1)
            pool.memset(ones[:, :], 1.0).then_inc(consts, 1)
            pool.memset(eps_sb[:, :], EPS).then_inc(consts, 1)
            pool.iota(pri_i[:, :], [[-1, N]], base=N, channel_multiplier=0).then_inc(consts, 1)
            pool.wait_ge(consts, 5)
            pool.affine_select(out=ident[:, :], in_=ident[:, :], compare_op=ALU.not_equal, fill=1.0,
                               base=0, pattern=[[-1, P]], channel_multiplier=1).then_inc(consts, 1)

            def gathers(nb, first):
                pool.wait_ge(table_stored, nb * 16 + 16)
                for t in range(T):
                    pool.wait_ge(idx_ready, nb * T + t + 1)
                    if not (first and t < RING):
                        pool.wait_ge(agg_ready, nb * T + t + 1 - RING)
                    pool.sem_inc(gathers_begun, 1)
                    for s in range(SLOTS):
                        pool.indirect_dma_start(
                            out=gathered[:, t % RING, s * C:(s + 1) * C], out_offset=None,
                            in_=table, in_offset=bass.IndirectOffsetOnAxis(ap=idx[:, t, s:s + 1], axis=0),
                        ).then_inc(gather_done[t % RING], 16)

            pool.wait_ge(zero_stored, 16)
            gathers(0, True)
            with pool.Fori(0, B - 1) as b:
                gathers(b + 1, False)

        @block.scalar
        def _(act):
            act.preload_act_table_set("natural_log_exp_and_others")

            def layer_norm(src, dst, mv_, rstd_, shift_, b, mom, rr, sr, ready, k, per):
                act.wait_ge(mom, b * per + k + 1)
                act.activation(rstd_[:, :], mv_[:, :, 1], ACT.Ln, bias=eps_sb[:, 0:1]).then_inc(act_own, own.one())
                act.wait_ge(act_own, own.value)
                act.activation(rstd_[:, :], rstd_[:, :], ACT.Exp, scale=-0.5).then_inc(rr, 1)
                act.wait_ge(rr, b * per + k + 1)
                act.wait_ge(sr, b * per + k + 1)
                for t in range(T):
                    act.activation(dst[:, t, :], src[:, t, :], ACT.Relu, bias=shift_[:, t:t + 1],
                                   scale=rstd_[:, t:t + 1]).then_inc(ready, 1)

            def next_norm(nb):
                layer_norm(xin, h0, n_mv, n_rstd, n_shift, nb, n_moments, n_rstd_ready,
                           n_shift_ready, h0_ready, 0, 1)
                for f in range(2):
                    act.wait_ge(h0_turned, nb * 2 + f + 1)
                    act.activation(h0_t[:, f * 512:f * 512 + 512], ps_n[:, :], ACT.Copy)\
                        .then_inc(h0_t_ready, 1)

            def next_turn(nb):
                for f in range(2):
                    act.wait_ge(agg_turned, nb * 2 + f + 1)
                    act.activation(agg_t[:, f * 512:f * 512 + 512], ps_a[:, f, :], ACT.Copy)\
                        .then_inc(agg_t_ready, 1)

            def norm_and_turn(b, layer):
                layer_norm(xres, h, mv, rstd, shift, b, moments, rstd_ready,
                           shift_ready, h_ready, layer, 3)

            def turn(b, layer):
                for f in range(2):
                    act.wait_ge(h_turned, b * 6 + 2 * layer + f + 1)
                    act.activation(h_t[:, f * 512:f * 512 + 512], ps_a[:, f, :], ACT.Copy)\
                        .then_inc(h_t_ready, 1)

            def exps(b, g):
                H, Fd = GAT[g]
                act.wait_ge(dist_ready, b * 2 + g + 1)
                act.activation(v[g][:, :, :, Fd], dist[:, :, 0:H], ACT.Exp)
                act.activation(v[g][:, :, :, 2 * Fd + 1], dist[:, :, 0:H], ACT.Exp, scale=SLOPE)
                act.activation(beta[:, :, 0:H], reach[:, :, 0:H], ACT.Relu).then_inc(act_own, own.one())
                act.wait_ge(act_own, own.value)
                act.activation(beta[:, :, 0:H], beta[:, :, 0:H], ACT.Exp, scale=SLOPE - 1.0)\
                    .then_inc(exps_ready, 1)

            def split(b, g):
                for k in range(2):
                    if k == 0:
                        act.wait_ge(v_ready, b * 2 + g + 1)
                    else:
                        act.wait_ge(rest_ready, b * 2 + g + 1)
                    act.activation(vp[g][:, :, :, k, :], v[g], ACT.Copy).then_inc(part_ready, 1)

            def attention(b, has_next):
                nonlocal own
                own = Own()
                norm_and_turn(b, 0)
                for j in range(T):
                    act.wait_ge(mask_turned, b * T + j + 1)
                    act.activation(mask_t[:, j, :], mask_ps[j % 4], ACT.Identity, bias=ones[:, 0:1])\
                        .then_inc(mask_t_ready, 1)
                turn(b, 0)
                exps(b, 0)
                if has_next:
                    next_norm(b + 1)
                split(b, 0)
                for t in range(T):
                    act.wait_ge(out1_done, b * T + t + 1)
                    if t >= 2:
                        act.wait_ge(x2_ready, b * T + t - 1)
                    act.activation(o1[:, t % 2, :], ps_a[:, t % 2, 0:3 * (C + 1)], ACT.Copy)\
                        .then_inc(o1_ready, 1)
                norm_and_turn(b, 1)
                turn(b, 1)
                act.wait_ge(hp_t_done, b + 1)
                act.activation(hp_t, wide_a, ACT.Identity, bias=cols[:, 0:1]).then_inc(hp_t_ready, 1)
                act.wait_ge(qk_done, b * 2 + 1)
                act.activation(q_t, wide_e[0], ACT.Identity, bias=cols[:, 3:4], scale=SLOPE * SCORE_SCALE)\
                    .then_inc(qk_ready, 1)
                act.wait_ge(qk_done, b * 2 + 2)
                act.activation(k_t, wide_e[1], ACT.Identity, bias=cols[:, 2:3]).then_inc(qk_ready, 1)
                act.wait_ge(hp_done, b + 1)
                act.activation(hp, tiles_a, ACT.Copy).then_inc(hp_ready, 1)
                for t in range(T + 2):
                    if t < T:
                        act.wait_ge(scores_done, b * T + t + 1)
                        if t >= 2:
                            act.wait_ge(masked_ready, b * T + t - 1)
                        act.activation(e_relu[t % 2], wide_e[t % 2], ACT.Relu, scale=(1.0 - SLOPE) / SLOPE)\
                            .then_inc(relu_ready, 1)
                    if 1 <= t <= T:
                        u = t - 1
                        act.wait_ge(neg_max_ready, b * T + u + 1)
                        act.activation(e_sb[u % 2], e_sb[u % 2], ACT.Exp, bias=neg_max[:, u:u + 1],
                                       accum_out=row_sum[:, u:u + 1]).then_inc(probs_ready, 1)
                    if t >= 2:
                        u = t - 2
                        act.wait_ge(probs_turned, b * T + u + 1)
                        if u >= 2:
                            act.wait_ge(out2_done, b * T + u - 1)
                        act.activation(p_t[u % 2], wide_a, ACT.Copy).then_inc(probs_t_ready, 1)
                norm_and_turn(b, 2)
                turn(b, 2)
                exps(b, 1)
                split(b, 1)
                if has_next:
                    next_turn(b + 1)
                act.wait_ge(act_own, own.value)
                act.sem_clear(act_own)

            own = Own()
            act.wait_ge(consts, 6)
            act.wait_ge(weights_in, N_WEIGHTS)
            next_norm(0)
            act.wait_ge(act_own, own.value)
            act.sem_clear(act_own)
            next_turn(0)
            with act.Fori(0, B - 1) as b:
                attention(b, True)
            attention(B - 1, False)

        @block.tensor
        def _(pe):
            def rows(t):
                return slice(t * P, t * P + P)

            def next_turn_features(nb, first):
                for f in range(2):
                    pe.wait_ge(h0_ready, nb * T + HALF * (f + 1))
                    if f == 0 and not first:
                        pe.wait_ge(x3_ready, (nb - 1) * T)
                    if f:
                        pe.wait_ge(h0_t_ready, nb * 2 + 1)
                    for t in range(HALF):
                        last = pe.transpose(ps_n[:, rows(t)], h0[:, HALF * f + t, :], ident[:, :])
                    last.then_inc(h0_turned, 1)

            def next_finish(nb):
                for f in range(2):
                    pe.wait_ge(agg_ready, nb * T + HALF * (f + 1))
                    for t in range(HALF):
                        last = pe.transpose(ps_a[:, f, rows(t)], agg[:, HALF * f + t, :], ident[:, :])
                    last.then_inc(agg_turned, 1)
                pe.wait_ge(h0_t_ready, nb * 2 + 2)
                for f in range(2):
                    pe.wait_ge(agg_t_ready, nb * 2 + f + 1)
                    for t in range(HALF):
                        o = ps_e[:, f, rows(t)]
                        tile = rows(HALF * f + t)
                        pe.matmul(o, h0_t[:, tile], w0_sb[:, 0, :], start=True, stop=False)
                        pe.matmul(o, agg_t[:, tile], w0_sb[:, 1, :], start=False, stop=False)
                        last = pe.matmul(o, ones[0:1, :], b0_sb[:, :], start=False, stop=True)
                    last.then_inc(linear_done, 1)

            def turn(b, layer):
                for f in range(2):
                    pe.wait_ge(h_ready, b * 3 * T + T * layer + HALF * (f + 1))
                    for t in range(HALF):
                        last = pe.transpose(ps_a[:, f, rows(t)], h[:, HALF * f + t, :], ident[:, :])
                    last.then_inc(h_turned, 1)

            def wide(o, lhs, rhs):
                for f in range(2):
                    last = pe.matmul(o[:, f * 512:f * 512 + 512], lhs, rhs[:, f * 512:f * 512 + 512],
                                     start=True, stop=True)
                return last

            def project(b, g):
                H, Fd = GAT[g]
                pe.wait_ge(h_t_ready, b * 6 + 4 * g + 2)
                wide(wide_a[0:H, :], wcat[g][:, C + H:C + 2 * H], h_t).then_inc(dst_done, 1)
                for t in range(T):
                    last = pe.matmul(slots_e[:, t, 0:C + 2 * H], h_t[:, rows(t)], wcat[g][:, 0:C + 2 * H],
                                     start=True, stop=True)
                last.then_inc(wh_done, 1)
                pe.wait_ge(diag_ready, b * 2 + g + 1)
                pe.matmul(ps_m[:, 0:H], ones[0:H, :], dmax_diag[0:H, 0:H], start=True, stop=True)\
                    .then_inc(dmax_spread, 1)

            def spread_source(b, g, head):
                k = head if g == 0 else 1 + head
                if head < 2:
                    pe.wait_ge(v_ready, b * 2 + g + 1)
                else:
                    pe.wait_ge(pos_ready, b * T * (1 + HEADS) + T * k - T)
                wide(wide_e[head % 2], src_bc[:, k, :], h_t).then_inc(src_spread, 1)

            def attention(b, has_next):
                turn(b, 0)
                for j in range(T):
                    if j >= 4:
                        pe.wait_ge(mask_t_ready, b * T + j - 3)
                    for t in range(T):
                        if j == 0:
                            pe.wait_ge(nmask_ready, b * T + t + 1)
                        last = pe.transpose(mask_ps[j % 4][:, rows(t)], nmask[:, t, rows(j)], identb[:, :])
                    last.then_inc(mask_turned, 1)
                pe.wait_ge(mask_t_ready, b * T + T)
                project(b, 0)
                spread_source(b, 0, 0)
                if has_next:
                    next_turn_features(b + 1, False)
                pe.wait_ge(parts_done, b * 2 + 1)
                pe.wait_ge(pos_ready, b * T * (1 + HEADS) + T)
                W = C + 1
                for t in range(T):
                    if t >= 2:
                        pe.wait_ge(o1_ready, b * T + t - 1)
                    o = ps_a[:, t % 2, :]
                    for n in range(3 * T):
                        j, k = n // 3, n % 3
                        pe.matmul(o[:, 0:2 * W], pos[:, 0, j, rows(t)], vp[0][:, j, 0, k, :],
                                  start=(n == 0), stop=(n == 3 * T - 1))
                    for n in range(3 * T):
                        j, k = n // 3, n % 3
                        last = pe.matmul(o[:, 2 * W:3 * W], mask_t[:, j, rows(t)], vp[0][:, j, 0, k, W:2 * W],
                                         start=(n == 0), stop=(n == 3 * T - 1))
                    last.then_inc(out1_done, 1)
                turn(b, 1)
                pe.wait_ge(h_t_ready, b * 6 + 4)
                wide(wide_a, ww_sb[:, :], h_t).then_inc(hp_t_done, 1)
                pe.wait_ge(hp_t_ready, b + 1)
                wide(wide_e[0], qw_sb[:, :], hp_t).then_inc(qk_done, 1)
                wide(wide_e[1], kw_sb[:, :], hp_t).then_inc(qk_done, 1)
                for t in range(T):
                    pe.matmul(tiles_a[:, t, :], h_t[:, rows(t)], ww_sb[:, :], start=True, stop=False)
                    last = pe.matmul(tiles_a[:, t, :], ones[0:1, :], wb_row[:, :], start=False, stop=True)
                last.then_inc(hp_done, 1)
                pe.wait_ge(qk_ready, b * 2 + 2)
                for t in range(T + 2):
                    if t < T:
                        if t >= 2:
                            pe.wait_ge(masked_ready, b * T + t - 1)
                        for f in range(2):
                            o, c = wide_e[t % 2][:, f * 512:f * 512 + 512], slice(f * 512, f * 512 + 512)
                            pe.matmul(o, q_t[:, rows(t)], k_t[:, c], start=True, stop=False)
                            last = pe.matmul(o, ident_big[:, :], nmask[:, t, c], start=False, stop=True)
                        last.then_inc(scores_done, 1)
                    if 1 <= t <= T:
                        u = t - 1
                        pe.wait_ge(probs_ready, b * T + u + 1)
                        if u == 0:
                            pe.wait_ge(hp_ready, b + 1)
                        else:
                            pe.wait_ge(probs_t_ready, b * T + u)
                        for j in range(T):
                            last = pe.transpose(tiles_a[:, j, :], e_sb[u % 2][:, rows(j)], ident[:, :])
                        last.then_inc(probs_turned, 1)
                    if t >= 2:
                        u = t - 2
                        pe.wait_ge(probs_t_ready, b * T + u + 1)
                        if u >= 2:
                            pe.wait_ge(x3_ready, b * T + u - 1)
                        elif u == 1 and has_next:
                            pe.wait_ge(h0_t_ready, (b + 1) * 2 + 2)
                        for j in range(T):
                            last = pe.matmul((ps_m, ps_n)[u % 2][:, 0:C], p_t[u % 2][:, rows(j)], hp[:, j, :],
                                             start=(j == 0), stop=(j == T - 1))
                        last.then_inc(out2_done, 1)
                turn(b, 2)
                project(b, 1)
                spread_source(b, 1, 0)
                spread_source(b, 1, 1)
                pe.wait_ge(parts_done, b * 2 + 2)
                W = HD + 1
                for t in range(T):
                    if t:
                        pe.wait_ge(all_ready, b * T + t)
                    for j in range(T):
                        last = pe.matmul(ps_m[:, 0:3 * HEADS * W], mask_t[:, j, rows(t)],
                                         vp[1][:, j, :, :, W:2 * W].rearrange("p h k w -> p (h k) w"),
                                         start=(j == 0), stop=(j == T - 1))
                    last.then_inc(all_done, 1)
                for head in range(HEADS):
                    pe.wait_ge(pos_ready, b * T * (1 + HEADS) + T * (2 + head))
                    if head + 2 < HEADS:
                        spread_source(b, 1, head + 2)
                    if head:
                        pe.wait_ge(head_ready, b * HEADS + head)
                    for t in range(T):
                        for j in range(T):
                            last = pe.matmul(tiles_a[:, t, 0:6 * W], pos[:, head % 2, j, rows(t)],
                                             vp[1][:, j, head, :, :].rearrange("p k w -> p (k w)"),
                                             start=(j == 0), stop=(j == T - 1))
                    last.then_inc(head_done, 1)
                if has_next:
                    pe.wait_ge(head_ready, b * HEADS + HEADS)
                    next_finish(b + 1)

            pe.wait_ge(consts, 6)
            pe.wait_ge(weights_in, N_WEIGHTS)
            pe.matmul(ps_m[:, 0:2], w1_sb[:, :], a1_sb[:, :], start=True, stop=True).then_inc(setup_pe, 1)
            next_turn_features(0, True)
            next_finish(0)
            pe.wait_ge(setup_v, 8)
            with pe.Fori(0, B - 1) as b:
                attention(b, True)
            attention(B - 1, False)

        @block.vector
        def _(dve):
            def moments_of(src, st_, mv_, own_sem, own, mom):
                for t in range(T):
                    dve.bn_stats(st_[:, t, :], src[:, t, :]).then_inc(own_sem, own.one())
                dve.wait_ge(own_sem, own.value)
                for t in range(T):
                    last = dve.bn_aggr(mv_[:, t, :], st_[:, t, :])
                last.then_inc(mom, 1)

            def shift_of(mv_, rstd_, shift_, b, k, per, rr, sr):
                dve.wait_ge(rr, b * per + k + 1)
                dve.scalar_tensor_tensor(out=shift_[:, :], in0=mv_[:, :, 0], scalar=-1.0, in1=rstd_[:, :],
                                         op0=ALU.mult, op1=ALU.mult).then_inc(sr, 1)

            def top(nb, own, t):
                if t % 2 == 0:
                    dve.wait_ge(adj_loaded[t // 2], nb * 16 + 16)
                dve.scalar_tensor_tensor(out=score[:, :], in0=adj_sb[:, t, :], scalar=0.0, in1=pri_i[:, :],
                                         op0=ALU.not_equal, op1=ALU.mult).then_inc(v_next, own.one())
                dve.wait_ge(v_next, own.value)
                for r in range(TOP // 8):
                    best = vals[:, t, 8 * r:8 * r + 8]
                    last = dve.max(best, score[:, :])
                    last.then_inc(v_next, own.one())
                    dve.wait_ge(v_next, own.value)
                    if r < TOP // 8 - 1:
                        dve.match_replace(score[:, :], best, score[:, :], 0.0).then_inc(v_next, own.one())
                        dve.wait_ge(v_next, own.value)
                dve.tensor_scalar(idx[:, t, :], vals[:, t, :], -1.0, float(N), ALU.mult, ALU.add)\
                    .then_inc(idx_ready, 1)

            def reduce(nb, t):
                if t == 0:
                    dve.wait_ge(h0_turned, nb * 2 + 2)
                dve.wait_ge(gather_done[t % RING], nb * GATHER_SIGNALS + 16 * SLOTS * (t // RING + 1))
                dve.tensor_reduce(agg[:, t, :], gathered[:, t % RING, :].rearrange("p (s c) -> p c s", s=SLOTS),
                                  AX.X, ALU.max).then_inc(agg_ready, 1)

            def next_finish(nb):
                for f in range(2):
                    dve.wait_ge(linear_done, nb * 2 + f + 1)
                    s = slice(HALF * f, HALF * f + HALF)
                    dve.scalar_tensor_tensor(out=xres[:, s, :], in0=ps_e[:, f, :].rearrange("p (t c) -> p t c", c=C),
                                             scalar=0.0, in1=xin[:, s, :], op0=ALU.max, op1=ALU.add)\
                        .then_inc(x1_ready, 1)

            def spread_max(b, g):
                H, Fd = GAT[g]
                dve.wait_ge(dst_done, b * 2 + g + 1)
                dve.tensor_reduce(dmax[0:H, :], wide_a[0:H, :], AX.X, ALU.max).then_inc(v_att, ch.one())
                dve.wait_ge(v_att, ch.value)
                dve.tensor_scalar(dmax_diag[0:H, 0:H], ident[0:H, 0:H], dmax[0:H, 0:1], None, ALU.mult)\
                    .then_inc(diag_ready, 1)

            def values(b, g):
                H, Fd = GAT[g]
                dve.wait_ge(dmax_spread, b * 2 + g + 1)
                dve.tensor_copy(dmax_all[:, 0:H], ps_m[:, 0:H]).then_inc(v_att, ch.one())
                dve.wait_ge(v_att, ch.value)
                top_d = dmax_all[:, 0:H].unsqueeze(1).broadcast_to([P, T, H])
                dve.wait_ge(wh_done, b * 2 + g + 1)
                src, dst = slots_e[:, :, C:C + H], slots_e[:, :, C + H:C + 2 * H]
                dve.tensor_tensor(reach[:, :, 0:H], src, top_d, ALU.add)
                dve.tensor_scalar(neg_dst[:, :, 0:H], dst, -1.0, None, ALU.mult).then_inc(v_att, ch.one())
                dve.tensor_tensor(dist[:, :, 0:H], dst, top_d, ALU.subtract).then_inc(dist_ready, 1)
                dve.wait_ge(exps_ready, b * 2 + g + 1)
                wh = slots_e[:, :, 0:C].rearrange("p t (h f) -> p t h f", h=H)
                for half in range(2):
                    at = half * (Fd + 1)
                    e = v[g][:, :, :, at + Fd:at + Fd + 1].broadcast_to([P, T, H, Fd])
                    if H == 1:
                        last = dve.tensor_tensor(v[g][:, :, 0, at:at + Fd], wh[:, :, 0, :], e[:, :, 0, :], ALU.mult)
                    else:
                        last = dve.tensor_tensor(v[g][:, :, :, at:at + Fd], wh, e, ALU.mult)
                last.then_inc(v_ready, 1)

            def split(b, g):
                dve.wait_ge(part_ready, b * 4 + 2 * g + 1)
                dve.wait_ge(v_ready, b * 2 + g + 1)
                dve.tensor_tensor(v[g], v[g], vp[g][:, :, :, 0, :], ALU.subtract).then_inc(rest_ready, 1)

            def split_last(b, g):
                dve.wait_ge(part_ready, b * 4 + 2 * g + 2)
                dve.tensor_tensor(vp[g][:, :, :, 2, :], v[g], vp[g][:, :, :, 1, :], ALU.subtract)\
                    .then_inc(parts_done, 1)

            def positive(b, g, head, j):
                k = head if g == 0 else 1 + head
                if j == 0:
                    dve.wait_ge(src_spread, b * (1 + HEADS) + k + 1)
                    if g and head >= 2:
                        dve.wait_ge(head_done, b * HEADS + head - 1)
                dve.scalar_tensor_tensor(out=pos[:, head % 2, j, :], in0=wide_e[head % 2],
                                         scalar=neg_dst[:, j, head:head + 1], in1=mask_t[:, j, :],
                                         op0=ALU.is_gt, op1=ALU.mult).then_inc(pos_ready, 1)

            def combine1(b, t):
                W = C + 1
                dve.wait_ge(o1_ready, b * T + t + 1)
                o, tot = o1[:, t % 2, :], o1_tot[:, t % 2, :]
                dve.tensor_tensor(tot, o[:, 2 * W:3 * W], o[:, W:2 * W], ALU.subtract).then_inc(v_att, ch.one())
                dve.wait_ge(v_att, ch.value)
                dve.scalar_tensor_tensor(out=tot, in0=tot, scalar=beta[:, t, 0:1], in1=o[:, 0:W],
                                                 op0=ALU.mult, op1=ALU.add).then_inc(v_att, ch.one())
                dve.wait_ge(v_att, ch.value)
                dve.reciprocal(recip[:, t, 0:1], tot[:, C:W]).then_inc(v_att, ch.one())
                dve.wait_ge(v_att, ch.value)
                dve.scalar_tensor_tensor(out=xres[:, t, :], in0=tot[:, 0:C], scalar=recip[:, t, 0:1],
                                         in1=xres[:, t, :], op0=ALU.mult, op1=ALU.add).then_inc(x2_ready, 1)

            def masked_max(b, t):
                dve.wait_ge(relu_ready, b * T + t + 1)
                if t >= 2:
                    dve.wait_ge(probs_turned, b * T + t - 1)
                dve.sem_inc(masking_begun, 1)
                dve.tensor_tensor_reduce(out=e_sb[t % 2], in0=wide_e[t % 2], in1=e_relu[t % 2], scale=1.0,
                                         scalar=-3.0e38, op0=ALU.add, op1=ALU.max,
                                         accum_out=row_max[:, t:t + 1]).then_inc(masked_ready, 1)
                dve.wait_ge(masked_ready, b * T + t + 1)
                dve.tensor_scalar(neg_max[:, t:t + 1], row_max[:, t:t + 1], -1.0, None, ALU.mult)\
                    .then_inc(neg_max_ready, 1)

            def combine2(b, t):
                dve.wait_ge(out2_done, b * T + t + 1)
                dve.reciprocal(recip[:, t, 0:1], row_sum[:, t:t + 1]).then_inc(v_att, ch.one())
                dve.wait_ge(v_att, ch.value)
                dve.tensor_scalar(o2[:, t % 2, :], (ps_m, ps_n)[t % 2][:, 0:C], 0.0,
                                          recip[:, t, 0:1], ALU.max, ALU.mult).then_inc(v_att, ch.one())
                dve.wait_ge(v_att, ch.value)
                dve.tensor_tensor(xres[:, t, :], xres[:, t, :], o2[:, t % 2, :], ALU.add)\
                    .then_inc(x3_ready, 1)

            def sum_all(b, t):
                dve.wait_ge(all_done, b * T + t + 1)
                W = HD + 1
                dve.tensor_reduce(all_out[:, t, :, :],
                                          ps_m[:, 0:3 * HEADS * W].rearrange("p (h k w) -> p h w k", h=HEADS, k=3),
                                          AX.X, ALU.add).then_inc(v_att, ch.one())
                dve.wait_ge(v_att, ch.value)
                dve.sem_inc(all_ready, 1)

            def sum_head(b, head):
                dve.wait_ge(head_done, b * HEADS + head + 1)
                W = 2 * (HD + 1)
                dve.tensor_reduce(head_out[:, head, :, :],
                                  tiles_a[:, :, 0:3 * W].rearrange("p t (k w) -> p t w k", k=3),
                                  AX.X, ALU.add).then_inc(head_ready, 1)

            def combine3(b):
                W = HD + 1
                dve.wait_ge(head_ready, b * HEADS + HEADS)
                plus = head_out[:, :, :, 0:W].rearrange("p h t w -> p t h w")
                minus = head_out[:, :, :, W:2 * W].rearrange("p h t w -> p t h w")
                a = all_out[:, :, :, :]
                dve.tensor_tensor(a, a, minus, ALU.subtract).then_inc(v_att, ch.one())
                dve.wait_ge(v_att, ch.value)
                dve.tensor_tensor(a, a, beta[:, :, :].unsqueeze(3).broadcast_to([P, T, HEADS, W]), ALU.mult).then_inc(v_att, ch.one())
                dve.wait_ge(v_att, ch.value)
                dve.tensor_tensor(a, a, plus, ALU.add).then_inc(v_att, ch.one())
                dve.wait_ge(v_att, ch.value)
                dve.reciprocal(recip[:, :, :], a[:, :, :, HD]).then_inc(v_att, ch.one())
                dve.wait_ge(v_att, ch.value)
                n = a[:, :, :, 0:HD]
                dve.tensor_tensor(n, n, recip[:, :, :].unsqueeze(3).broadcast_to([P, T, HEADS, HD]), ALU.mult).then_inc(v_att, ch.one())
                dve.wait_ge(v_att, ch.value)
                dve.wait_ge(stored, b * 16)
                dve.tensor_tensor(outb[:, :, :].rearrange("p t (h f) -> p t h f", h=HEADS), n,
                                  xres[:, :, :].rearrange("p t (h f) -> p t h f", h=HEADS), ALU.add)\
                    .then_inc(x4_ready, 1)

            def attention(b, has_next):
                nonlocal ch
                ch = Own()
                nxt = Own()
                tops, sums = iter(range(T)), iter(range(T))

                def run_top():
                    if has_next:
                        top(b + 1, nxt, next(tops))

                def run_sum():
                    if has_next:
                        reduce(b + 1, next(sums))

                dve.wait_ge(x1_ready, b * 2 + 2)
                moments_of(xres, st, mv, v_att, ch, moments)
                for t in range(T):
                    if t == HALF:
                        shift_of(mv, rstd, shift, b, 0, 3, rstd_ready, shift_ready)
                    dve.tensor_scalar(nmask[:, t, :], adj_sb[:, t, :], 0.0, -1.0, ALU.not_equal, ALU.add)\
                        .then_inc(nmask_ready, 1)
                if has_next:
                    dve.wait_ge(x_loaded, (b + 1) * 16 + 16)
                    moments_of(xin, n_st, n_mv, v_next, nxt, n_moments)
                spread_max(b, 0)
                values(b, 0)
                if has_next:
                    shift_of(n_mv, n_rstd, n_shift, b + 1, 0, 1, n_rstd_ready, n_shift_ready)
                run_top()
                split(b, 0)
                dve.wait_ge(mask_t_ready, b * T + T)
                for j in range(T):
                    positive(b, 0, 0, j)
                split_last(b, 0)
                run_top()
                for t in range(T):
                    combine1(b, t)
                dve.wait_ge(x2_ready, b * T + T)
                moments_of(xres, st, mv, v_att, ch, moments)
                shift_of(mv, rstd, shift, b, 1, 3, rstd_ready, shift_ready)
                run_top()
                for t in range(T + 2):
                    if t < T:
                        masked_max(b, t)
                    if t >= 2:
                        combine2(b, t - 2)
                    if t == 2:
                        run_sum()
                    if t == 6:
                        run_top()
                dve.wait_ge(x3_ready, b * T + T)
                moments_of(xres, st, mv, v_att, ch, moments)
                shift_of(mv, rstd, shift, b, 2, 3, rstd_ready, shift_ready)
                run_sum()
                spread_max(b, 1)
                values(b, 1)
                split(b, 1)
                run_top()
                split_last(b, 1)
                for head in range(HEADS):
                    for j in range(T):
                        positive(b, 1, head, j)
                        if head == 0:
                            sum_all(b, j)
                    if head:
                        sum_head(b, head - 1)
                    if head in (1, 3, 5, 6, 7):
                        run_sum()
                    if head in (0, 2, 4):
                        run_top()
                sum_head(b, HEADS - 1)
                combine3(b)
                dve.wait_ge(v_att, ch.value)
                dve.sem_clear(v_att)
                if has_next:
                    run_sum()
                    dve.wait_ge(v_next, nxt.value)
                    dve.sem_clear(v_next)
                    next_finish(b + 1)

            ch = None
            dve.wait_ge(consts, 6)
            dve.wait_ge(weights_in, N_WEIGHTS)
            sv = setup_v
            dve.tensor_copy(identb[:, :], ident[:, :]).then_inc(sv, 1)
            dve.tensor_scalar(ident_big[:, :], ident[:, :], MASKED, None, ALU.mult).then_inc(sv, 1)
            dve.tensor_scalar(cols[:, 3:4], cols[:, 1:2], SLOPE * SCORE_SCALE, None, ALU.mult).then_inc(sv, 1)
            for k in range(2):
                dve.tensor_tensor(a3_prod[:, :, :], wcat[1][:, 0:C].rearrange("p (h f) -> p h f", h=HEADS),
                                  a3_sb[:, k * HD:(k + 1) * HD].unsqueeze(1).broadcast_to([P, HEADS, HD]),
                                  ALU.mult).then_inc(sv, 1)
                dve.wait_ge(sv, 4 + 2 * k)
                dve.tensor_reduce(wcat[1][:, C + k * HEADS:C + (k + 1) * HEADS], a3_prod[:, :, :], AX.X, ALU.add)\
                    .then_inc(sv, 1)
                dve.wait_ge(sv, 5 + 2 * k)
            dve.wait_ge(setup_pe, 1)
            dve.tensor_copy(wcat[0][:, C:C + 2], ps_m[:, 0:2]).then_inc(sv, 1)
            dve.wait_ge(sv, 8)
            dve.tensor_copy(src_bc[:, 0, :], wcat[0][:, C:C + 1].broadcast_to([P, P]))
            dve.tensor_copy(src_bc[:, 1:1 + HEADS, :],
                            wcat[1][:, C:C + HEADS].unsqueeze(2).broadcast_to([P, HEADS, P])).then_inc(sv, 1)

            nxt0 = Own()
            dve.wait_ge(x_loaded, 16)
            moments_of(xin, n_st, n_mv, v_next, nxt0, n_moments)
            shift_of(n_mv, n_rstd, n_shift, 0, 0, 1, n_rstd_ready, n_shift_ready)
            for t in range(T):
                top(0, nxt0, t)
                if t >= RING:
                    reduce(0, t - RING)
            for t in range(T - RING, T):
                reduce(0, t)
            dve.wait_ge(v_next, nxt0.value)
            dve.sem_clear(v_next)
            next_finish(0)
            with dve.Fori(0, B - 1) as b:
                attention(b, True)
            attention(B - 1, False)


_OUT = (8, 1024, 128)


def kernel(**inputs):
    import numpy as np
    import concourse.bacc as bacc
    from concourse import mybir as mb
    from concourse.bass_utils import run_bass_kernel_spmd

    def arr(name):
        return np.asarray(inputs[name])

    laid = {
        "x": arr("x"), "adj": arr("adj"), "w0": arr("L0_gnn_W"), "b0": arr("L0_gnn_b"),
        "w1": arr("L1_gnn_W"), "w1_t": arr("L1_gnn_W").T, "a1": arr("L1_gnn_a").reshape(2, 128).T,
        "ww_t": arr("L2_gnn_W_w").T, "wb": arr("L2_gnn_W_b"),
        "qw_t": arr("L2_gnn_Q_w").T, "qb": arr("L2_gnn_Q_b"),
        "kw_t": arr("L2_gnn_K_w").T, "kb": arr("L2_gnn_K_b"),
        "w3": arr("L3_gnn_W"), "a3": np.broadcast_to(arr("L3_gnn_a"), (128, 32)),
    }
    nc = bacc.Bacc("TRN2", target_bir_lowering=False, num_devices=1)
    arrays, args = {}, []
    for name, a in laid.items():
        a = np.ascontiguousarray(a)
        arrays[f"in_{name}"] = a
        args.append(nc.dram_tensor(f"in_{name}", a.shape, mb.dt.from_np(a.dtype), kind="ExternalInput").ap())
    args.append(nc.dram_tensor("out_x", _OUT, mb.dt.float32, kind="ExternalOutput").ap())
    graph_layers_kernel(nc, *args)
    r = run_bass_kernel_spmd(nc, [arrays], core_ids=[0])
    return r.results[0]["out_x"]
```

```python
import concourse.bass as bass
from concourse import mybir
from contextlib import ExitStack

F32 = mybir.dt.float32
BF16 = mybir.dt.bfloat16
I32 = mybir.dt.int32
U32 = mybir.dt.uint32
ALU = mybir.AluOpType
ACT = mybir.ActivationFunctionType
AX = mybir.AxisListType

P = 128
SLOTS = 25
TOP = 32
FEW = 18
SEGMENTS = 8
EPS = 1e-5
SLOPE = 0.2
MASKED = 1.0e9
STEEP = 1.0e20


class Own:

    def __init__(self):
        self.value = 0

    def one(self):
        self.value += 1
        return 1


def graph_layers_kernel(nc, x, adj, w0, b0, w1, w1_t, a1, ww_t, wb, qw_t, qb, kw_t, kb, w3, a3, out):
    B, N, C = x.shape
    T = N // P
    HALF = T // 2
    HEADS = 8
    HD = C // HEADS
    GAT = [(1, C), (HEADS, HD)]
    WH = C + 2 * HEADS
    SCORE_SCALE = 1.0 / float(C) ** 0.5
    RING = 2

    x_d = x.rearrange("b (t p) c -> b p t c", p=P)
    adj_d = adj.rearrange("b (t p) j -> b p t j", p=P)
    out_d = out.rearrange("b (t p) c -> b p t c", p=P)
    tables = [nc.dram_tensor(f"feature_table{i}", [N + 1, C], F32, kind="Internal").ap() for i in range(2)]
    table_rows = [table[0:N, :].rearrange("(t p) c -> p t c", p=P) for table in tables]

    with ExitStack() as ctx:
        def sb(name, shape, dt=F32):
            return ctx.enter_context(nc.sbuf_tensor(name, shape, dt))

        def ps(name, shape, dt=F32):
            return ctx.enter_context(nc.psum_tensor(name, shape, dt))

        def sem(name):
            return ctx.enter_context(nc.semaphore(name))

        w0_sb = sb("w0_sb", [P, 2, C])
        b0_sb = sb("b0_sb", [1, C])
        w1_sb = sb("w1_sb", [P, C])
        a1_sb = sb("a1_sb", [P, 2])
        wcat = [sb("wcat1", [P, C + 2]), sb("wcat3", [P, C + 2 * HEADS])]
        src_bc = sb("src_bc", [P, 1 + HEADS, P])
        ww_sb = sb("ww_sb", [P, C])
        qw_sb = sb("qw_sb", [P, C])
        kw_sb = sb("kw_sb", [P, C])
        wb_row = sb("wb_row", [1, C])
        cols = sb("cols", [P, 4])
        a3_sb = sb("a3_sb", [P, 2 * HD])
        a3_prod = sb("a3_prod", [P, HEADS, HD])
        ident = sb("ident", [P, P])
        identb = sb("identb", [P, P], BF16)
        ident_big = sb("ident_big", [P, P], BF16)
        ones = sb("ones", [P, P])
        eps_sb = sb("eps_sb", [P, 1])
        pri_i = sb("pri_i", [P, N], mybir.dt.int16)
        zero_row = sb("zero_row", [1, C])

        adj_sb = sb("adj_sb", [P, T, N], I32)
        xin = sb("xin", [P, T, C])
        h0 = sb("h0", [P, T, C])
        h0_t = sb("h0_t", [P, N])
        agg = sb("agg", [P, T, C])
        score = sb("score", [P, N], mybir.dt.float16)
        best_in = sb("best_in", [P, 2, SEGMENTS * 8], mybir.dt.float16)
        vals = sb("vals", [P, 2, TOP])
        flag = sb("flag", [P, 32])
        flag_t = sb("flag_t", [P, 32])
        crowded = sb("crowded", [P, 1], I32)
        many = sb("many", [P, HALF], I32)
        idx = sb("idx", [P, T, TOP], U32)
        gathered = sb("gathered", [P, RING, SLOTS * C])
        n_st = sb("n_st", [P, T, 6])
        n_mv = sb("n_mv", [P, T, 2])
        n_rstd = sb("n_rstd", [P, T])
        n_shift = sb("n_shift", [P, T])

        x1 = sb("x1", [P, T, C])
        xres = sb("xres", [P, T, C])
        h = sb("h", [P, T, C])
        h_t = sb("h_t", [P, N])
        agg_t = sb("agg_t", [P, N])
        st = sb("st", [P, T, 6])
        mv = sb("mv", [P, T, 2])
        rstd = sb("rstd", [P, T])
        shift = sb("shift", [P, T])
        nmask = sb("nmask", [P, T, N], BF16)
        mask_t = sb("mask_t", [P, T, N], BF16)
        pos = sb("pos", [P, 2, T, N], BF16)
        v_words = T * HEADS * 2 * (HD + 1)
        v_sb = sb("v_sb", [P, v_words])
        vp_sb = sb("vp_sb", [P, 3 * v_words], BF16)
        v = [v_sb[:, 0:T * 2 * (C + 1)].rearrange("p (t h w) -> p t h w", t=T, h=1),
             v_sb[:, :].rearrange("p (t h w) -> p t h w", t=T, h=HEADS)]
        vp = [vp_sb[:, 0:T * 6 * (C + 1)].rearrange("p (t h k w) -> p t h k w", t=T, h=1, k=3),
              vp_sb[:, :].rearrange("p (t h k w) -> p t h k w", t=T, h=HEADS, k=3)]
        dmax = sb("dmax", [HEADS, 1])
        dmax_diag = sb("dmax_diag", [HEADS, HEADS])
        dmax_all = sb("dmax_all", [P, HEADS])
        dist = sb("dist", [P, T, HEADS])
        big_dst = sb("big_dst", [P, T, HEADS])
        reach = sb("reach", [P, T, HEADS])
        beta = sb("beta", [P, T, HEADS])
        o1 = sb("o1", [P, 2, 2 * (C + 1)])
        o1_tot = sb("o1_tot", [P, 2, C + 1])
        recip = sb("recip", [P, T, HEADS])
        head_out = v_sb[:, :].rearrange("p (h t w) -> p h t w", h=HEADS, t=T)
        all_out = sb("all_out", [P, T, HEADS, HD + 1])
        pos_f = pos[:, :, :, :].rearrange("p a t n -> p (a t n)").bitcast(F32)
        e_relu = [pos_f[:, i * N:(i + 1) * N] for i in (0, 1)]
        e_sb = [pos_f[:, i * N:(i + 1) * N] for i in (2, 3)]
        p_t = [pos_f[:, i * N:(i + 1) * N] for i in (4, 5)]
        hp_t = pos_f[:, 6 * N:7 * N]
        hp = pos_f[:, 7 * N:8 * N].rearrange("p (t c) -> p t c", t=T)
        q_t = v_sb[:, 0:N]
        k_t = v_sb[:, N:2 * N]
        row_max = sb("row_max", [P, T])
        neg_max = sb("neg_max", [P, T])
        row_sum = sb("row_sum", [P, T])
        o2 = sb("o2", [P, 2, C])

        ps_e = ps("ps_e", [P, 4, 512])
        ps_a = ps("ps_a", [P, 2, 512])
        ps_m = ps("ps_m", [P, 512])
        ps_n = ps("ps_n", [P, 512])
        wide_e = [ps_e[:, 2 * i:2 * i + 2, :].rearrange("p b w -> p (b w)") for i in (0, 1)]
        wide_a = ps_a[:, :, :].rearrange("p b w -> p (b w)")
        tiles_a = wide_a.rearrange("p (t w) -> p t w", t=T)
        mask_ps = [ps_e[:, i, :].bitcast(BF16) for i in range(2)]
        wh_banks = [(0, 3, ps_a[:, 0, :]), (3, 6, ps_a[:, 1, :]), (6, 8, ps_m[:, :])]

        GATHER_SIGNALS = 16 * FEW * T // RING
        weights_in = sem("weights_in")
        consts = sem("consts")
        setup_v = sem("setup_v")
        setup_pe = sem("setup_pe")
        x_loaded = sem("x_loaded")
        residual_loaded = sem("residual_loaded")
        requests_begun = sem("requests_begun")
        adj_loaded = [sem(f"adj_loaded{q}") for q in range(4)]
        table_stored = sem("table_stored")
        n_moments = sem("n_moments")
        n_rstd_ready = sem("n_rstd_ready")
        n_shift_ready = sem("n_shift_ready")
        h0_ready = sem("h0_ready")
        h0_turned = sem("h0_turned")
        h0_t_ready = sem("h0_t_ready")
        idx_ready = sem("idx_ready")
        gather_done = [sem(f"gather_done{r}") for r in range(RING)]
        more_done = sem("more_done")
        rest_done = [sem(f"rest_done{r}") for r in range(RING)]
        gathers_begun = sem("gathers_begun")
        agg_ready = sem("agg_ready")
        agg_turned = sem("agg_turned")
        agg_t_ready = sem("agg_t_ready")
        linear_done = sem("linear_done")
        x1_ready = sem("x1_ready")
        v_next = sem("v_next")

        nmask_ready = sem("nmask_ready")
        mask_turned = sem("mask_turned")
        mask_t_ready = sem("mask_t_ready")
        moments = sem("moments")
        act_own = sem("act_own")
        rstd_ready = sem("rstd_ready")
        shift_ready = sem("shift_ready")
        h_ready = sem("h_ready")
        h_turned = sem("h_turned")
        h_t_ready = sem("h_t_ready")
        wh_done = sem("wh_done")
        dst_done = sem("dst_done")
        diag_ready = sem("diag_ready")
        dmax_spread = sem("dmax_spread")
        dist_ready = sem("dist_ready")
        exps_ready = sem("exps_ready")
        v_ready = sem("v_ready")
        part_ready = sem("part_ready")
        rest_ready = sem("rest_ready")
        parts_done = sem("parts_done")
        src_spread = sem("src_spread")
        ramp_ready = sem("ramp_ready")
        pos_ready = sem("pos_ready")
        out1_done = sem("out1_done")
        o1_ready = sem("o1_ready")
        x2_ready = sem("x2_ready")
        hp_t_done = sem("hp_t_done")
        hp_t_ready = sem("hp_t_ready")
        qk_done = sem("qk_done")
        qk_ready = sem("qk_ready")
        hp_done = sem("hp_done")
        hp_ready = sem("hp_ready")
        scores_done = sem("scores_done")
        relu_ready = sem("relu_ready")
        masking_begun = sem("masking_begun")
        masked_ready = sem("masked_ready")
        neg_max_ready = sem("neg_max_ready")
        probs_ready = sem("probs_ready")
        probs_turned = sem("probs_turned")
        probs_t_ready = sem("probs_t_ready")
        out2_done = sem("out2_done")
        x3_ready = sem("x3_ready")
        all_done = sem("all_done")
        all_ready = sem("all_ready")
        head_done = sem("head_done")
        head_ready = sem("head_ready")
        x4_ready = sem("x4_ready")
        stored = sem("stored")
        v_att = sem("v_att")
        v_search = sem("v_search")

        N_WEIGHTS = 14 * 16
        ZERO_ROWS = 2 * 16
        AGG_TURN, AGG_COPY, AGG_LINEAR = (0, 4), (2, 6), (2, 6)
        FAR_NORM = 3

        block = ctx.enter_context(nc.Block())

        @block.sync
        def _(sp):
            loads = [(w0_sb[:, :, :], w0.rearrange("(k p) o -> p k o", p=P)),
                     (b0_sb[:, :], b0.rearrange("(a n) -> a n", a=1)),
                     (w1_sb[:, :], w1), (wcat[0][:, 0:C], w1_t),
                     (a1_sb[:, :], a1),
                     (ww_sb[:, :], ww_t), (qw_sb[:, :], qw_t), (kw_sb[:, :], kw_t),
                     (wb_row[:, :], wb.rearrange("(a n) -> a n", a=1)),
                     (cols[:, 0:1], wb.rearrange("(p a) -> p a", a=1)),
                     (cols[:, 1:2], qb.rearrange("(p a) -> p a", a=1)),
                     (cols[:, 2:3], kb.rearrange("(p a) -> p a", a=1)),
                     (wcat[1][:, 0:C], w3), (a3_sb[:, :], a3)]

            def load_x(nb):
                sp.dma_start(xin[:, :, :], x_d[nb]).then_inc(x_loaded, 16)

            def load_adj(nb, q):
                sp.dma_start(adj_sb[:, 2 * q:2 * q + 2, :], adj_d[nb, :, 2 * q:2 * q + 2, :])\
                    .then_inc(adj_loaded[q], 16)

            def load_adj_next(nb):
                for q in range(4):
                    sp.wait_ge(nmask_ready, nb * T - T + 2 * q + 2)
                    sp.sem_inc(requests_begun, 1)
                    load_adj(nb, q)

            def load_x_next(nb):
                sp.wait_ge(h0_ready, nb * T)
                sp.sem_inc(requests_begun, 1)
                load_x(nb)

            def load_residual(nb, first):
                if not first:
                    sp.wait_ge(x2_ready, nb * T)
                    sp.sem_inc(requests_begun, 1)
                sp.dma_start(x1[:, :, :], x_d[nb]).then_inc(residual_loaded, 16)

            def store_table(nb, parity, first=False):
                sp.wait_ge(h0_ready, nb * T + T)
                sp.sem_inc(requests_begun, 1)
                if not first:
                    sp.wait_ge(agg_ready, nb * T - T)
                    sp.sem_inc(requests_begun, 1)
                sp.dma_start(table_rows[parity], h0[:, :, :]).then_inc(table_stored, 16)

            def store_out(b):
                sp.wait_ge(x4_ready, b + 1)
                sp.sem_inc(requests_begun, 1)
                sp.dma_start(out_d[b], xres[:, :, :]).then_inc(stored, 16)

            load_x(0)
            for q in range(4):
                load_adj(0, q)
            for dst, src in loads:
                sp.dma_start(dst, src).then_inc(weights_in, 16)
            load_residual(0, True)
            sp.wait_ge(consts, 1)
            for table in tables:
                sp.dma_start(table[N:N + 1, :], zero_row[:, :]).then_inc(stored, 16)
            store_table(0, 0, True)
            load_x_next(1)
            load_adj_next(1)
            store_table(1, 1, True)
            with sp.Fori(0, B - 3, 2) as even:
                for parity in range(2):
                    b = even + parity
                    load_x_next(b + 2)
                    load_residual(b + 1, False)
                    load_adj_next(b + 2)
                    store_table(b + 2, parity)
                    store_out(b)
            load_residual(B - 1, False)
            store_out(B - 2)
            store_out(B - 1)
            sp.wait_ge(stored, ZERO_ROWS + B * 16)

        @block.gpsimd
        def _(pool):
            pool.memset(zero_row[:, :], 0.0).then_inc(consts, 1)
            pool.memset(ident[:, :], 0.0).then_inc(consts, 1)
            pool.memset(ones[:, :], 1.0).then_inc(consts, 1)
            pool.memset(flag[:, :], 0.0).then_inc(consts, 1)
            pool.memset(eps_sb[:, :], EPS).then_inc(consts, 1)
            pool.iota(pri_i[:, :], [[-1, N]], base=N, channel_multiplier=0).then_inc(consts, 1)
            pool.wait_ge(consts, 6)
            pool.affine_select(out=ident[:, :], in_=ident[:, :], compare_op=ALU.not_equal, fill=1.0,
                               base=0, pattern=[[-1, P]], channel_multiplier=1).then_inc(consts, 1)

            def gathers(nb, parity, first):
                pool.wait_ge(table_stored, nb * 16 + 16)
                for t in range(T):
                    pool.wait_ge(idx_ready, nb * HALF + t // 2 + 1)
                    if not (first and t < RING):
                        pool.wait_ge(agg_ready, nb * T + t + 1 - RING)
                    pool.sem_inc(gathers_begun, 1)

                    def gather(slots, done):
                        for s in slots:
                            pool.indirect_dma_start(
                                out=gathered[:, t % RING, s * C:(s + 1) * C], out_offset=None, in_=tables[parity],
                                in_offset=bass.IndirectOffsetOnAxis(ap=idx[:, t, s:s + 1], axis=0),
                            ).then_inc(done, 16)

                    gather(range(FEW), gather_done[t % RING])
                    more = sum(pool.value_load(many[k + t % 2:k + t % 2 + 1, t // 2:t // 2 + 1], min_val=0, max_val=N)
                               for k in range(0, P, 32))
                    with pool.If(more > 0):
                        gather(range(FEW, SLOTS), more_done)
                        pool.reg_add(more_count, more_count, 16 * (SLOTS - FEW))
                        pool.wait_ge(more_done, more_count)
                        pool.sem_inc(rest_done[t % RING], 1)
                    with pool.Else():
                        pool.memset(gathered[:, t % RING, FEW * C:SLOTS * C], 0.0)\
                            .then_inc(rest_done[t % RING], 1)

            pool.wait_ge(stored, ZERO_ROWS)
            more_count = pool.alloc_register("more_count")
            pool.reg_mov(more_count, 0)
            gathers(0, 0, True)
            with pool.Fori(0, B - 3, 2) as even:
                for parity in (1, 0):
                    gathers(even + 2 - parity, parity, False)
            gathers(B - 1, 1, False)

        @block.scalar
        def _(act):
            act.preload_act_table_set("natural_log_exp_and_others")

            def deviation(mv_, rstd_, b, mom, rr, k, per):
                act.wait_ge(mom, b * per + k + 1)
                act.activation(rstd_[:, :], mv_[:, :, 1], ACT.Ln, bias=eps_sb[:, 0:1]).then_inc(act_own, own.one())
                act.wait_ge(act_own, own.value)
                act.activation(rstd_[:, :], rstd_[:, :], ACT.Exp, scale=-0.5).then_inc(rr, 1)

            def normalise(src, dst, rstd_, shift_, b, rr, sr, ready, k, per):
                act.wait_ge(rr, b * per + k + 1)
                act.wait_ge(sr, b * per + k + 1)
                for t in range(T):
                    act.activation(dst[:, t, :], src[:, t, :], ACT.Relu, bias=shift_[:, t:t + 1],
                                   scale=rstd_[:, t:t + 1]).then_inc(ready, 1)

            def next_deviation(nb):
                deviation(n_mv, n_rstd, nb, n_moments, n_rstd_ready, 0, 1)

            def next_norm(nb, first):
                if not first:
                    act.wait_ge(table_stored, nb * 16)
                normalise(xin, h0, n_rstd, n_shift, nb, n_rstd_ready, n_shift_ready, h0_ready, 0, 1)

            def next_turn_features(nb):
                for f in range(2):
                    act.wait_ge(h0_turned, nb * 2 + f + 1)
                    act.activation(h0_t[:, f * 512:f * 512 + 512], (ps_n, ps_m)[f][:, :], ACT.Copy)\
                        .then_inc(h0_t_ready, 1)

            def next_turn(nb, f):
                act.wait_ge(agg_turned, nb * 2 + f + 1)
                act.activation(agg_t[:, f * 512:f * 512 + 512], ps_n[:, :], ACT.Copy)\
                    .then_inc(agg_t_ready, 1)

            def norm(b, layer):
                deviation(mv, rstd, b, moments, rstd_ready, layer, 3)
                normalise(xres if layer else x1, h, rstd, shift, b, rstd_ready, shift_ready, h_ready, layer, 3)

            def turn(b, layer):
                for f in range(2):
                    act.wait_ge(h_turned, b * 6 + 2 * layer + f + 1)
                    act.activation(h_t[:, f * 512:f * 512 + 512], ps_a[:, f, :] if layer else (ps_n, ps_m)[f][:, :],
                                   ACT.Copy).then_inc(h_t_ready, 1)

            def exps(b, g):
                H, Fd = GAT[g]
                act.wait_ge(dist_ready, b * 2 + g + 1)
                act.activation(v[g][:, :, :, Fd], dist[:, :, 0:H], ACT.Exp)
                act.activation(v[g][:, :, :, 2 * Fd + 1], dist[:, :, 0:H], ACT.Exp, scale=SLOPE)
                act.activation(beta[:, :, 0:H], reach[:, :, 0:H], ACT.Relu).then_inc(act_own, own.one())
                act.wait_ge(act_own, own.value)
                act.activation(beta[:, :, 0:H], beta[:, :, 0:H], ACT.Exp, scale=SLOPE - 1.0)\
                    .then_inc(exps_ready, 1)

            def split(b, g, k):
                if k == 0:
                    act.wait_ge(v_ready, b * 2 + g + 1)
                else:
                    act.wait_ge(rest_ready, b * 2 + g + 1)
                act.activation(vp[g][:, :, :, k, :], v[g], ACT.Copy).then_inc(part_ready, 1)

            def ramps(b, g, head, js):
                k = head if g == 0 else 1 + head
                act.wait_ge(src_spread, b * (1 + HEADS) + k + 1)
                if g and head >= 2:
                    act.wait_ge(head_done, b * HEADS + head - 1)
                for j in js:
                    act.activation(pos[:, head % 2, j, :], wide_e[head % 2 if g else 1], ACT.Relu,
                                   bias=big_dst[:, j, head:head + 1], scale=STEEP).then_inc(ramp_ready, 1)

            def turn_mask(b, j):
                act.wait_ge(mask_turned, b * T + j + 1)
                act.activation(mask_t[:, j, :], mask_ps[j % 2], ACT.Identity, bias=ones[:, 0:1])\
                    .then_inc(mask_t_ready, 1)

            def attention(b, has_next, has_far):
                nonlocal own
                own = Own()
                for j in range(4):
                    turn_mask(b, j)
                exps(b, 0)
                ramps(b, 0, 0, (0, 1))
                split(b, 0, 0)
                for j in (4, 5):
                    turn_mask(b, j)
                split(b, 0, 1)
                for j in (6, 7):
                    turn_mask(b, j)
                ramps(b, 0, 0, range(2, T))
                if has_next:
                    next_turn_features(b + 1)
                for t in range(T):
                    act.wait_ge(out1_done, b * T + t + 1)
                    if t >= 2:
                        act.wait_ge(x2_ready, b * T + t - 1)
                    act.activation(o1[:, t % 2, :], ps_a[:, t % 2, 0:2 * (C + 1)], ACT.Copy)\
                        .then_inc(o1_ready, 1)
                norm(b, 1)
                turn(b, 1)
                act.wait_ge(hp_t_done, b + 1)
                act.activation(hp_t, wide_a, ACT.Identity, bias=cols[:, 0:1]).then_inc(hp_t_ready, 1)
                act.wait_ge(qk_done, b * 2 + 1)
                act.activation(q_t, wide_e[0], ACT.Identity, bias=cols[:, 3:4], scale=SLOPE * SCORE_SCALE)\
                    .then_inc(qk_ready, 1)
                act.wait_ge(qk_done, b * 2 + 2)
                act.activation(k_t, wide_e[1], ACT.Identity, bias=cols[:, 2:3]).then_inc(qk_ready, 1)
                act.wait_ge(hp_done, b + 1)
                act.activation(hp, tiles_a, ACT.Copy).then_inc(hp_ready, 1)
                for t in range(T + 1):
                    if t:
                        act.wait_ge(neg_max_ready, b * T + t)
                        act.activation(e_sb[(t - 1) % 2], e_sb[(t - 1) % 2], ACT.Exp, bias=neg_max[:, t - 1:t],
                                       accum_out=row_sum[:, t - 1:t]).then_inc(probs_ready, 1)
                    if t < T:
                        act.wait_ge(scores_done, b * T + t + 1)
                        if t >= 2:
                            act.wait_ge(masked_ready, b * T + t - 1)
                        act.activation(e_relu[t % 2], wide_e[t % 2], ACT.Relu, scale=(1.0 - SLOPE) / SLOPE)\
                            .then_inc(relu_ready, 1)
                    if t:
                        act.wait_ge(probs_turned, b * T + t)
                        if t > 2:
                            act.wait_ge(out2_done, b * T + t - 2)
                        act.activation(p_t[(t - 1) % 2], wide_a, ACT.Copy).then_inc(probs_t_ready, 1)
                norm(b, 2)
                turn(b, 2)
                exps(b, 1)
                ramps(b, 1, 0, range(0, 2))
                split(b, 1, 0)
                ramps(b, 1, 0, range(2, 5))
                split(b, 1, 1)
                ramps(b, 1, 0, range(5, T))
                for head in range(1, HEADS):
                    ramps(b, 1, head, range(T))
                    if has_next and head in AGG_COPY:
                        next_turn(b + 1, AGG_COPY.index(head))
                    if has_far and head == FAR_NORM:
                        next_deviation(b + 2)
                    if has_far and head == FAR_NORM + 1:
                        next_norm(b + 2, False)
                if has_next:
                    norm(b + 1, 0)
                    turn(b + 1, 0)
                act.wait_ge(act_own, own.value)
                act.sem_clear(act_own)

            own = Own()
            act.wait_ge(consts, 7)
            act.wait_ge(weights_in, N_WEIGHTS)
            next_deviation(0)
            next_norm(0, True)
            next_turn_features(0)
            next_deviation(1)
            next_norm(1, False)
            for f in range(2):
                next_turn(0, f)
            norm(0, 0)
            turn(0, 0)
            act.wait_ge(act_own, own.value)
            act.sem_clear(act_own)
            with act.Fori(0, B - 2) as b:
                attention(b, True, True)
            attention(B - 2, True, False)
            attention(B - 1, False, False)

        @block.tensor
        def _(pe):
            def rows(t):
                return slice(t * P, t * P + P)

            def next_turn_features(nb, first):
                if not first:
                    pe.wait_ge(v_ready, nb * 2 - 1)
                for f in range(2):
                    pe.wait_ge(h0_ready, nb * T + HALF * (f + 1))
                    for t in range(HALF):
                        last = pe.transpose((ps_n, ps_m)[f][:, rows(t)], h0[:, HALF * f + t, :], ident[:, :])
                    last.then_inc(h0_turned, 1)

            def next_turn(nb, f):
                pe.wait_ge(agg_ready, nb * T + HALF * (f + 1))
                if f:
                    pe.wait_ge(x1_ready, nb * 2 + 1)
                for t in range(HALF):
                    last = pe.transpose(ps_n[:, rows(t)], agg[:, HALF * f + t, :], ident[:, :])
                last.then_inc(agg_turned, 1)

            def next_linear(nb, f):
                pe.wait_ge(h0_t_ready, nb * 2 + 2)
                pe.wait_ge(agg_t_ready, nb * 2 + f + 1)
                for t in range(HALF):
                    o, tile = ps_n[:, rows(t)], rows(HALF * f + t)
                    pe.matmul(o, h0_t[:, tile], w0_sb[:, 0, :], start=True, stop=False)
                    pe.matmul(o, agg_t[:, tile], w0_sb[:, 1, :], start=False, stop=False)
                    last = pe.matmul(o, ones[0:1, :], b0_sb[:, :], start=False, stop=True)
                last.then_inc(linear_done, 1)

            def turn(b, layer):
                for f in range(2):
                    pe.wait_ge(h_ready, b * 3 * T + T * layer + HALF * (f + 1))
                    o = ps_a[:, f, :] if layer else (ps_n, ps_m)[f][:, :]
                    for t in range(HALF):
                        last = pe.transpose(o[:, rows(t)], h[:, HALF * f + t, :], ident[:, :])
                    last.then_inc(h_turned, 1)

            def wide(o, lhs, rhs):
                for f in range(2):
                    last = pe.matmul(o[:, f * 512:f * 512 + 512], lhs, rhs[:, f * 512:f * 512 + 512],
                                     start=True, stop=True)
                return last

            def project(b, g):
                H, Fd = GAT[g]
                pe.wait_ge(h_t_ready, b * 6 + 4 * g + 2)
                wide(wide_e[1][0:H, :], wcat[g][:, C + H:C + 2 * H], h_t).then_inc(dst_done, 1)
                for t0, t1, bank in wh_banks:
                    for t in range(t0, t1):
                        o = bank[:, (t - t0) * WH:(t - t0) * WH + C + 2 * H]
                        last = pe.matmul(o, h_t[:, rows(t)], wcat[g][:, 0:C + 2 * H], start=True, stop=True)
                last.then_inc(wh_done, 1)

            def spread_max(b, g):
                H, Fd = GAT[g]
                pe.wait_ge(diag_ready, b * 2 + g + 1)
                pe.matmul(ps_n[:, 0:H], ones[0:H, :], dmax_diag[0:H, 0:H], start=True, stop=True)\
                    .then_inc(dmax_spread, 1)

            def spread_source(b, g, head):
                k = head if g == 0 else 1 + head
                if head >= 2:
                    pe.wait_ge(ramp_ready, b * T * (1 + HEADS) + T * k - T)
                wide(wide_e[head % 2 if g else 1], src_bc[:, k, :], h_t).then_inc(src_spread, 1)

            def turn_mask(b, j):
                if j >= 2:
                    pe.wait_ge(mask_t_ready, b * T + j - 1)
                for t in range(T):
                    if j == 0:
                        pe.wait_ge(nmask_ready, b * T + t + 1)
                    last = pe.transpose(mask_ps[j % 2][:, rows(t)], nmask[:, t, rows(j)], identb[:, :])
                last.then_inc(mask_turned, 1)

            def attention(b, has_next, has_far):
                project(b, 0)
                for j in range(4):
                    turn_mask(b, j)
                spread_max(b, 0)
                spread_source(b, 0, 0)
                for j in range(4, T):
                    turn_mask(b, j)
                if has_next:
                    next_turn_features(b + 1, False)
                pe.wait_ge(parts_done, b * 2 + 1)
                pe.wait_ge(pos_ready, b * T * (1 + HEADS) + T)
                W = C + 1
                for t in range(T):
                    if t >= 2:
                        pe.wait_ge(o1_ready, b * T + t - 1)
                    for part in range(2):
                        o = ps_a[:, t % 2, part * W:part * W + W]
                        for n in range(3 * T):
                            j, k = n // 3, n % 3
                            last = pe.matmul(o, pos[:, part, j, rows(t)], vp[0][:, j, 0, k, part * W:part * W + W],
                                             start=(n == 0), stop=(n == 3 * T - 1))
                    last.then_inc(out1_done, 1)
                turn(b, 1)
                pe.wait_ge(h_t_ready, b * 6 + 4)
                wide(wide_a, ww_sb[:, :], h_t).then_inc(hp_t_done, 1)
                pe.wait_ge(hp_t_ready, b + 1)
                wide(wide_e[0], qw_sb[:, :], hp_t).then_inc(qk_done, 1)
                wide(wide_e[1], kw_sb[:, :], hp_t).then_inc(qk_done, 1)
                for t in range(T):
                    pe.matmul(tiles_a[:, t, :], h_t[:, rows(t)], ww_sb[:, :], start=True, stop=False)
                    last = pe.matmul(tiles_a[:, t, :], ones[0:1, :], wb_row[:, :], start=False, stop=True)
                last.then_inc(hp_done, 1)
                pe.wait_ge(qk_ready, b * 2 + 2)
                for t in range(T + 2):
                    if t < T:
                        if t >= 2:
                            pe.wait_ge(masked_ready, b * T + t - 1)
                        for f in range(2):
                            o, c = wide_e[t % 2][:, f * 512:f * 512 + 512], slice(f * 512, f * 512 + 512)
                            pe.matmul(o, q_t[:, rows(t)], k_t[:, c], start=True, stop=False)
                            last = pe.matmul(o, ident_big[:, :], nmask[:, t, c], start=False, stop=True)
                        last.then_inc(scores_done, 1)
                    if 1 <= t <= T:
                        u = t - 1
                        pe.wait_ge(probs_ready, b * T + u + 1)
                        if u == 0:
                            pe.wait_ge(hp_ready, b + 1)
                        else:
                            pe.wait_ge(probs_t_ready, b * T + u)
                        for j in range(T):
                            last = pe.transpose(tiles_a[:, j, :], e_sb[u % 2][:, rows(j)], ident[:, :])
                        last.then_inc(probs_turned, 1)
                    if t >= 2:
                        u = t - 2
                        pe.wait_ge(probs_t_ready, b * T + u + 1)
                        if u >= 2:
                            pe.wait_ge(x3_ready, b * T + u - 1)
                        elif u == 0 and has_next:
                            pe.wait_ge(h0_t_ready, (b + 1) * 2 + 2)
                        for j in range(T):
                            last = pe.matmul((ps_m, ps_n)[u % 2][:, 0:C], p_t[u % 2][:, rows(j)], hp[:, j, :],
                                             start=(j == 0), stop=(j == T - 1))
                        last.then_inc(out2_done, 1)
                turn(b, 2)
                project(b, 1)
                spread_max(b, 1)
                spread_source(b, 1, 0)
                spread_source(b, 1, 1)
                pe.wait_ge(parts_done, b * 2 + 2)
                W = HD + 1
                for head in range(HEADS):
                    pe.wait_ge(pos_ready, b * T * (1 + HEADS) + T * (2 + head))
                    if head:
                        pe.wait_ge(head_ready, b * HEADS + head)
                    for t in range(T):
                        for j in range(T):
                            last = pe.matmul(tiles_a[:, t, 0:6 * W], pos[:, head % 2, j, rows(t)],
                                             vp[1][:, j, head, :, :].rearrange("p k w -> p (k w)"),
                                             start=(j == 0), stop=(j == T - 1))
                    last.then_inc(head_done, 1)
                    if head + 2 < HEADS:
                        spread_source(b, 1, head + 2)
                    if head:
                        pe.wait_ge(all_ready, b * T + head)
                    for j in range(T):
                        last = pe.matmul(ps_m[:, 0:3 * HEADS * W], mask_t[:, j, rows(head)],
                                         vp[1][:, j, :, :, W:2 * W].rearrange("p h k w -> p (h k) w"),
                                         start=(j == 0), stop=(j == T - 1))
                    last.then_inc(all_done, 1)
                    if has_next and head in AGG_LINEAR:
                        next_linear(b + 1, AGG_LINEAR.index(head))
                    if has_next and head in AGG_TURN:
                        next_turn(b + 1, AGG_TURN.index(head))
                if has_next:
                    pe.wait_ge(all_ready, b * T + T)
                    pe.wait_ge(head_ready, b * HEADS + HEADS)
                    pe.wait_ge(x1_ready, b * 2 + 4)
                    turn(b + 1, 0)

            pe.wait_ge(consts, 7)
            pe.wait_ge(weights_in, N_WEIGHTS)
            pe.matmul(ps_e[:, 3, 0:2], w1_sb[:, :], a1_sb[:, :], start=True, stop=True).then_inc(setup_pe, 1)
            next_turn_features(0, True)
            for f in range(2):
                if f == 0:
                    pe.wait_ge(h0_t_ready, 2)
                next_turn(0, f)
                next_linear(0, f)
            pe.wait_ge(x1_ready, 2)
            turn(0, 0)
            pe.wait_ge(setup_v, 9)
            with pe.Fori(0, B - 2) as b:
                attention(b, True, True)
            attention(B - 2, True, False)
            attention(B - 1, False, False)

        @block.vector
        def _(dve):
            def moments_of(src, st_, mv_, own_sem, own, mom):
                for t in range(T):
                    dve.bn_stats(st_[:, t, :], src[:, t, :]).then_inc(own_sem, own.one())
                dve.wait_ge(own_sem, own.value)
                for t in range(T):
                    last = dve.bn_aggr(mv_[:, t, :], st_[:, t, :])
                last.then_inc(mom, 1)

            def shift_of(mv_, rstd_, shift_, b, k, per, rr, sr):
                dve.wait_ge(rr, b * per + k + 1)
                dve.scalar_tensor_tensor(out=shift_[:, :], in0=mv_[:, :, 0], scalar=-1.0, in1=rstd_[:, :],
                                         op0=ALU.mult, op1=ALU.mult).then_inc(sr, 1)

            def score_of(t):
                return dve.scalar_tensor_tensor(out=score[:, :], in0=adj_sb[:, t, :], scalar=0.0, in1=pri_i[:, :],
                                                op0=ALU.not_equal, op1=ALU.mult)

            def segment_tops(nb, own, q, i):
                if own.value:
                    dve.wait_ge(v_next, own.value)
                if i == 0:
                    dve.wait_ge(adj_loaded[q], nb * 16 + 16)
                score_of(2 * q + i).then_inc(v_next, own.one())
                dve.wait_ge(v_next, own.value)
                for g in range(SEGMENTS):
                    width = N // SEGMENTS
                    last = dve.max(best_in[:, i, 8 * g:8 * g + 8], score[:, width * g:width * g + width])
                last.then_inc(v_next, own.one())

            def over_rows(own, out):
                dve.wait_ge(v_next, own.value)
                dve.transpose(flag_t[:, :], flag[:, :]).then_inc(v_next, own.one())
                dve.wait_ge(v_next, own.value)
                dve.tensor_reduce(out, flag_t[:, :], AX.X, ALU.max).then_inc(v_next, own.one())

            def settle_crowds(own, q):
                dve.wait_ge(v_next, own.value)
                dve.tensor_reduce(flag[:, 0:1], best_in[:, :, 7:SEGMENTS * 8:8], AX.XY, ALU.max)\
                    .then_inc(v_next, own.one())
                over_rows(own, crowded[:, :])
                dve.wait_ge(v_next, own.value)
                crowds = sum(dve.value_load(crowded[k:k + 1, 0:1], min_val=0, max_val=N) for k in range(0, P, 32))
                with dve.If(crowds > 0):
                    searched = Own()
                    for i in range(2):
                        score_of(2 * q + i).then_inc(v_search, searched.one())
                        dve.memset(best_in[:, i, TOP:], 0.0)
                        dve.wait_ge(v_search, searched.value)
                        for r in range(TOP // 8):
                            best = best_in[:, i, 8 * r:8 * r + 8]
                            dve.max(best, score[:, :]).then_inc(v_search, searched.one())
                            dve.wait_ge(v_search, searched.value)
                            if r < TOP // 8 - 1:
                                dve.tensor_copy(vals[:, i, 8 * r:8 * r + 8], best).then_inc(v_search, searched.one())
                                dve.wait_ge(v_search, searched.value)
                                dve.match_replace(score[:, :], vals[:, i, 8 * r:8 * r + 8], score[:, :], 0.0)\
                                    .then_inc(v_search, searched.one())
                                dve.wait_ge(v_search, searched.value)
                    dve.sem_clear(v_search)

            def tops(own, q):
                for i in range(2):
                    for r in range(TOP // 8):
                        best = vals[:, i, 8 * r:8 * r + 8]
                        dve.max(best, best_in[:, i, :]).then_inc(v_next, own.one())
                        dve.wait_ge(v_next, own.value)
                        if r < TOP // 8 - 1:
                            dve.match_replace(best_in[:, i, :], best, best_in[:, i, :], 0.0)\
                                .then_inc(v_next, own.one())
                            dve.wait_ge(v_next, own.value)
                dve.tensor_scalar(idx[:, 2 * q:2 * q + 2, :], vals[:, :, :], -1.0, float(N), ALU.mult, ALU.add)
                dve.tensor_copy(flag[:, 0:2], vals[:, :, FEW]).then_inc(v_next, own.one())
                over_rows(own, many[:, q:q + 1])
                dve.wait_ge(v_next, own.value)
                dve.sem_inc(idx_ready, 1)

            def top(nb, own, q, part):
                if part < 2:
                    segment_tops(nb, own, q, part)
                if part == 1:
                    settle_crowds(own, q)
                if part == 2:
                    tops(own, q)

            def reduce(nb, t):
                dve.wait_ge(gather_done[t % RING], nb * GATHER_SIGNALS + 16 * FEW * (t // RING + 1))
                dve.wait_ge(rest_done[t % RING], nb * (T // RING) + t // RING + 1)
                dve.tensor_reduce(agg[:, t, :], gathered[:, t % RING, :].rearrange("p (s c) -> p c s", s=SLOTS),
                                  AX.X, ALU.max).then_inc(agg_ready, 1)

            def next_finish(nb, f):
                dve.wait_ge(linear_done, nb * 2 + f + 1)
                dve.wait_ge(residual_loaded, nb * 16 + 16)
                s = slice(HALF * f, HALF * f + HALF)
                dve.scalar_tensor_tensor(out=x1[:, s, :], in0=ps_n[:, :].rearrange("p (t c) -> p t c", c=C),
                                         scalar=0.0, in1=x1[:, s, :], op0=ALU.max, op1=ALU.add)\
                    .then_inc(x1_ready, 1)

            def spread_max(b, g):
                H, Fd = GAT[g]
                dve.wait_ge(dst_done, b * 2 + g + 1)
                dve.tensor_reduce(dmax[0:H, :], wide_e[1][0:H, :], AX.X, ALU.max).then_inc(v_att, ch.one())
                dve.wait_ge(v_att, ch.value)
                dve.tensor_scalar(dmax_diag[0:H, 0:H], ident[0:H, 0:H], dmax[0:H, 0:1], None, ALU.mult)\
                    .then_inc(diag_ready, 1)

            def values(b, g):
                H, Fd = GAT[g]
                dve.wait_ge(dmax_spread, b * 2 + g + 1)
                dve.tensor_copy(dmax_all[:, 0:H], ps_n[:, 0:H]).then_inc(v_att, ch.one())
                dve.wait_ge(v_att, ch.value)
                dve.wait_ge(wh_done, b * 2 + g + 1)
                for t0, t1, bank in wh_banks:
                    node = bank[:, 0:(t1 - t0) * WH].rearrange("p (t w) -> p t w", w=WH)
                    src, dst = node[:, :, C:C + H], node[:, :, C + H:C + 2 * H]
                    top_d = dmax_all[:, 0:H].unsqueeze(1).broadcast_to([P, t1 - t0, H])
                    dve.tensor_tensor(reach[:, t0:t1, 0:H], src, top_d, ALU.add)
                    dve.tensor_scalar(big_dst[:, t0:t1, 0:H], dst, STEEP, None, ALU.mult)
                    last = dve.tensor_tensor(dist[:, t0:t1, 0:H], dst, top_d, ALU.subtract)
                last.then_inc(dist_ready, 1)
                dve.wait_ge(exps_ready, b * 2 + g + 1)
                for t0, t1, bank in wh_banks:
                    wh = bank[:, 0:(t1 - t0) * WH].rearrange("p (t w) -> p t w", w=WH)[:, :, 0:C]
                    for half in range(2):
                        at = half * (Fd + 1)
                        vt = v[g][:, t0:t1, :, :]
                        if H == 1:
                            e = vt[:, :, 0, at + Fd:at + Fd + 1].broadcast_to([P, t1 - t0, Fd])
                            last = dve.tensor_tensor(vt[:, :, 0, at:at + Fd], wh, e, ALU.mult)
                        else:
                            e = vt[:, :, :, at + Fd:at + Fd + 1].broadcast_to([P, t1 - t0, H, Fd])
                            last = dve.tensor_tensor(vt[:, :, :, at:at + Fd],
                                                     wh.rearrange("p t (h f) -> p t h f", h=H), e, ALU.mult)
                last.then_inc(v_ready, 1)

            def split(b, g):
                dve.wait_ge(part_ready, b * 4 + 2 * g + 1)
                dve.wait_ge(v_ready, b * 2 + g + 1)
                dve.tensor_tensor(v[g], v[g], vp[g][:, :, :, 0, :], ALU.subtract).then_inc(rest_ready, 1)

            def split_last(b, g):
                dve.wait_ge(part_ready, b * 4 + 2 * g + 2)
                dve.tensor_tensor(vp[g][:, :, :, 2, :], v[g], vp[g][:, :, :, 1, :], ALU.subtract)\
                    .then_inc(parts_done, 1)

            def positive(b, g, head, j):
                k = head if g == 0 else 1 + head
                dve.wait_ge(ramp_ready, b * T * (1 + HEADS) + k * T + j + 1)
                here = pos[:, head % 2, j, :]
                cut = dve.tensor_tensor(here, here, mask_t[:, j, :], ALU.min)
                if g:
                    cut.then_inc(pos_ready, 1)
                else:
                    cut.then_inc(v_att, ch.one())
                    dve.wait_ge(v_att, ch.value)
                    dve.tensor_tensor(pos[:, 1, j, :], mask_t[:, j, :], here, ALU.subtract).then_inc(pos_ready, 1)

            def combine1(b, t):
                W = C + 1
                dve.wait_ge(o1_ready, b * T + t + 1)
                if t == 0:
                    dve.wait_ge(stored, ZERO_ROWS + b * 16)
                o, tot = o1[:, t % 2, :], o1_tot[:, t % 2, :]
                dve.scalar_tensor_tensor(out=tot, in0=o[:, W:2 * W], scalar=beta[:, t, 0:1], in1=o[:, 0:W],
                                         op0=ALU.mult, op1=ALU.add).then_inc(v_att, ch.one())
                dve.wait_ge(v_att, ch.value)
                dve.reciprocal(recip[:, t, 0:1], tot[:, C:W]).then_inc(v_att, ch.one())
                dve.wait_ge(v_att, ch.value)
                dve.scalar_tensor_tensor(out=xres[:, t, :], in0=tot[:, 0:C], scalar=recip[:, t, 0:1],
                                         in1=x1[:, t, :], op0=ALU.mult, op1=ALU.add).then_inc(x2_ready, 1)

            def masked_max(b, t):
                dve.wait_ge(relu_ready, b * T + t + 1)
                if t >= 2:
                    dve.wait_ge(probs_turned, b * T + t - 1)
                dve.sem_inc(masking_begun, 1)
                dve.tensor_tensor_reduce(out=e_sb[t % 2], in0=wide_e[t % 2], in1=e_relu[t % 2], scale=1.0,
                                         scalar=-3.0e38, op0=ALU.add, op1=ALU.max,
                                         accum_out=row_max[:, t:t + 1]).then_inc(masked_ready, 1)
                dve.wait_ge(masked_ready, b * T + t + 1)
                dve.tensor_scalar(neg_max[:, t:t + 1], row_max[:, t:t + 1], -1.0, None, ALU.mult)\
                    .then_inc(neg_max_ready, 1)

            def combine2(b, t):
                dve.wait_ge(out2_done, b * T + t + 1)
                dve.reciprocal(recip[:, t, 0:1], row_sum[:, t:t + 1]).then_inc(v_att, ch.one())
                dve.wait_ge(v_att, ch.value)
                dve.tensor_scalar(o2[:, t % 2, :], (ps_m, ps_n)[t % 2][:, 0:C], 0.0,
                                          recip[:, t, 0:1], ALU.max, ALU.mult).then_inc(v_att, ch.one())
                dve.wait_ge(v_att, ch.value)
                dve.tensor_tensor(xres[:, t, :], xres[:, t, :], o2[:, t % 2, :], ALU.add)\
                    .then_inc(x3_ready, 1)

            def sum_all(b, t):
                dve.wait_ge(all_done, b * T + t + 1)
                W = HD + 1
                dve.tensor_reduce(all_out[:, t, :, :],
                                          ps_m[:, 0:3 * HEADS * W].rearrange("p (h k w) -> p h w k", h=HEADS, k=3),
                                          AX.X, ALU.add).then_inc(v_att, ch.one())
                dve.wait_ge(v_att, ch.value)
                dve.sem_inc(all_ready, 1)

            def sum_head(b, head):
                dve.wait_ge(head_done, b * HEADS + head + 1)
                W = 2 * (HD + 1)
                dve.tensor_reduce(head_out[:, head, :, :],
                                  tiles_a[:, :, 0:3 * W].rearrange("p t (k w) -> p t w k", k=3),
                                  AX.X, ALU.add).then_inc(head_ready, 1)

            def combine3(b):
                W = HD + 1
                dve.wait_ge(head_ready, b * HEADS + HEADS)
                plus = head_out[:, :, :, 0:W].rearrange("p h t w -> p t h w")
                minus = head_out[:, :, :, W:2 * W].rearrange("p h t w -> p t h w")
                a = all_out[:, :, :, :]
                dve.tensor_tensor(a, a, minus, ALU.subtract).then_inc(v_att, ch.one())
                dve.wait_ge(v_att, ch.value)
                dve.tensor_tensor(a, a, beta[:, :, :].unsqueeze(3).broadcast_to([P, T, HEADS, W]), ALU.mult).then_inc(v_att, ch.one())
                dve.wait_ge(v_att, ch.value)
                dve.tensor_tensor(a, a, plus, ALU.add).then_inc(v_att, ch.one())
                dve.wait_ge(v_att, ch.value)
                dve.reciprocal(recip[:, :, :], a[:, :, :, HD]).then_inc(v_att, ch.one())
                dve.wait_ge(v_att, ch.value)
                n = a[:, :, :, 0:HD]
                dve.tensor_tensor(n, n, recip[:, :, :].unsqueeze(3).broadcast_to([P, T, HEADS, HD]), ALU.mult).then_inc(v_att, ch.one())
                dve.wait_ge(v_att, ch.value)
                res = xres[:, :, :].rearrange("p t (h f) -> p t h f", h=HEADS)
                dve.tensor_tensor(res, n, res, ALU.add)\
                    .then_inc(x4_ready, 1)

            def mask_rows(nb, t):
                if t % 2 == 0:
                    dve.wait_ge(adj_loaded[t // 2], nb * 16 + 16)
                dve.tensor_scalar(nmask[:, t, :], adj_sb[:, t, :], 0.0, -1.0, ALU.not_equal, ALU.add)\
                    .then_inc(nmask_ready, 1)

            def next_moments(nb, own):
                dve.wait_ge(x_loaded, nb * 16 + 16)
                moments_of(xin, n_st, n_mv, v_next, own, n_moments)

            def next_shift(nb):
                shift_of(n_mv, n_rstd, n_shift, nb, 0, 1, n_rstd_ready, n_shift_ready)

            def first_moments(b, own_sem, own):
                dve.wait_ge(x1_ready, b * 2 + 2)
                moments_of(x1, st, mv, own_sem, own, moments)

            def first_shift(b):
                shift_of(mv, rstd, shift, b, 0, 3, rstd_ready, shift_ready)

            def attention(b, has_next, has_far):
                nonlocal ch
                ch = Own()
                nxt = Own()
                parts = iter([(t, part) for t in range(1, HALF) for part in range(3)])
                sums = iter(range(T))

                def run_top(n):
                    for _ in range(n if has_next else 0):
                        t, part = next(parts)
                        top(b + 1, nxt, t, part)

                def run_sum():
                    if has_next:
                        reduce(b + 1, next(sums))

                spread_max(b, 0)
                values(b, 0)
                dve.wait_ge(mask_t_ready, b * T + 2)
                for j in (0, 1):
                    positive(b, 0, 0, j)
                split(b, 0)
                run_top(1)
                split_last(b, 0)
                run_top(2)
                dve.wait_ge(mask_t_ready, b * T + T)
                for j in range(2, T):
                    positive(b, 0, 0, j)
                run_sum()
                for t in range(T):
                    if t in (0, 2, 4):
                        run_top(1)
                    combine1(b, t)
                    if t == 5:
                        run_sum()
                dve.wait_ge(x2_ready, b * T + T)
                moments_of(xres, st, mv, v_att, ch, moments)
                shift_of(mv, rstd, shift, b, 1, 3, rstd_ready, shift_ready)
                run_sum()
                for t in range(T + 2):
                    if t < T:
                        masked_max(b, t)
                    if t >= 2:
                        combine2(b, t - 2)
                    if t in (0, 2, 4):
                        run_top(1)
                    if t in (3, 7):
                        run_sum()
                dve.wait_ge(x3_ready, b * T + T)
                moments_of(xres, st, mv, v_att, ch, moments)
                shift_of(mv, rstd, shift, b, 2, 3, rstd_ready, shift_ready)
                if has_next:
                    for t in range(T):
                        mask_rows(b + 1, t)
                spread_max(b, 1)
                values(b, 1)
                for j in (0, 1):
                    positive(b, 1, 0, j)
                split(b, 1)
                for j in (2, 3, 4):
                    positive(b, 1, 0, j)
                split_last(b, 1)
                for head in range(HEADS):
                    for j in range(0 if head else 5, T):
                        positive(b, 1, head, j)
                    if head:
                        sum_head(b, head - 1)
                        sum_all(b, head - 1)
                    if head in (0, 2, 4):
                        run_sum()
                    if has_next and head - 1 in AGG_LINEAR:
                        next_finish(b + 1, AGG_LINEAR.index(head - 1))
                    if has_far:
                        if head == FAR_NORM - 1:
                            next_moments(b + 2, nxt)
                        if head == FAR_NORM:
                            next_shift(b + 2)
                        if head == 5:
                            top(b + 2, nxt, 0, 0)
                        if head == 6:
                            top(b + 2, nxt, 0, 1)
                        if head == 7:
                            top(b + 2, nxt, 0, 2)
                if has_next:
                    first_moments(b + 1, v_next, nxt)
                sum_head(b, HEADS - 1)
                sum_all(b, HEADS - 1)
                if has_next:
                    first_shift(b + 1)
                combine3(b)
                dve.wait_ge(v_att, ch.value)
                dve.sem_clear(v_att)
                if has_next:
                    dve.wait_ge(v_next, nxt.value)
                    dve.sem_clear(v_next)

            ch = None
            dve.wait_ge(consts, 7)
            dve.wait_ge(weights_in, N_WEIGHTS)
            sv = setup_v
            dve.tensor_copy(identb[:, :], ident[:, :]).then_inc(sv, 1)
            dve.tensor_scalar(ident_big[:, :], ident[:, :], MASKED, None, ALU.mult).then_inc(sv, 1)
            dve.tensor_scalar(cols[:, 3:4], cols[:, 1:2], SLOPE * SCORE_SCALE, None, ALU.mult).then_inc(sv, 1)
            for k in range(2):
                dve.tensor_tensor(a3_prod[:, :, :], wcat[1][:, 0:C].rearrange("p (h f) -> p h f", h=HEADS),
                                  a3_sb[:, k * HD:(k + 1) * HD].unsqueeze(1).broadcast_to([P, HEADS, HD]),
                                  ALU.mult).then_inc(sv, 1)
                dve.wait_ge(sv, 4 + 2 * k)
                dve.tensor_reduce(wcat[1][:, C + k * HEADS:C + (k + 1) * HEADS], a3_prod[:, :, :], AX.X, ALU.add)\
                    .then_inc(sv, 1)
                dve.wait_ge(sv, 5 + 2 * k)
            dve.wait_ge(setup_pe, 1)
            dve.tensor_copy(wcat[0][:, C:C + 2], ps_e[:, 3, 0:2]).then_inc(sv, 1)
            dve.wait_ge(sv, 8)
            dve.tensor_copy(src_bc[:, 0, :], wcat[0][:, C:C + 1].broadcast_to([P, P]))
            dve.tensor_copy(src_bc[:, 1:1 + HEADS, :],
                            wcat[1][:, C:C + HEADS].unsqueeze(2).broadcast_to([P, HEADS, P])).then_inc(sv, 1)

            nxt0 = Own()
            next_moments(0, nxt0)
            next_shift(0)
            for q in range(HALF):
                for part in range(3):
                    top(0, nxt0, q, part)
            for t in range(T):
                mask_rows(0, t)
            next_moments(1, nxt0)
            next_shift(1)
            for t in range(4):
                reduce(0, t)
            for part in range(3):
                top(1, nxt0, 0, part)
            for t in range(4, T):
                reduce(0, t)
            for f in range(2):
                next_finish(0, f)
            first_moments(0, v_next, nxt0)
            first_shift(0)
            dve.wait_ge(v_next, nxt0.value)
            dve.sem_clear(v_next)
            with dve.Fori(0, B - 2) as b:
                attention(b, True, True)
            attention(B - 2, True, False)
            attention(B - 1, False, False)


_OUT = (8, 1024, 128)


def kernel(**inputs):
    import numpy as np
    import concourse.bacc as bacc
    from concourse import mybir as mb
    from concourse.bass_utils import run_bass_kernel_spmd

    def arr(name):
        return np.asarray(inputs[name])

    laid = {
        "x": arr("x"), "adj": arr("adj"), "w0": arr("L0_gnn_W"), "b0": arr("L0_gnn_b"),
        "w1": arr("L1_gnn_W"), "w1_t": arr("L1_gnn_W").T, "a1": arr("L1_gnn_a").reshape(2, 128).T,
        "ww_t": arr("L2_gnn_W_w").T, "wb": arr("L2_gnn_W_b"),
        "qw_t": arr("L2_gnn_Q_w").T, "qb": arr("L2_gnn_Q_b"),
        "kw_t": arr("L2_gnn_K_w").T, "kb": arr("L2_gnn_K_b"),
        "w3": arr("L3_gnn_W"), "a3": np.broadcast_to(arr("L3_gnn_a"), (128, 32)),
    }
    nc = bacc.Bacc("TRN2", target_bir_lowering=False, num_devices=1)
    arrays, args = {}, []
    for name, a in laid.items():
        a = np.ascontiguousarray(a)
        arrays[f"in_{name}"] = a
        args.append(nc.dram_tensor(f"in_{name}", a.shape, mb.dt.from_np(a.dtype), kind="ExternalInput").ap())
    args.append(nc.dram_tensor("out_x", _OUT, mb.dt.float32, kind="ExternalOutput").ap())
    graph_layers_kernel(nc, *args)
    r = run_bass_kernel_spmd(nc, [arrays], core_ids=[0])
    return r.results[0]["out_x"]
```

```python
import concourse.bass as bass
from concourse import mybir
from contextlib import ExitStack

F32 = mybir.dt.float32
BF16 = mybir.dt.bfloat16
I32 = mybir.dt.int32
U32 = mybir.dt.uint32
ALU = mybir.AluOpType
ACT = mybir.ActivationFunctionType
AX = mybir.AxisListType

P = 128
SLOTS = 25
TOP = 32
FEW = 18
SEGMENTS = 8
EPS = 1e-5
SLOPE = 0.2
MASKED = 1.0e9
STEEP = 1.0e20


class Own:

    def __init__(self):
        self.value = 0

    def one(self):
        self.value += 1
        return 1


def graph_layers_kernel(nc, x, adj, w0, b0, w1, w1_t, a1, ww_t, wb, qw_t, qb, kw_t, kb, w3, a3, out):
    B, N, C = x.shape
    T = N // P
    HALF = T // 2
    HEADS = 8
    HD = C // HEADS
    GAT = [(1, C), (HEADS, HD)]
    WH = C + 2 * HEADS
    SCORE_SCALE = 1.0 / float(C) ** 0.5
    RING = 2

    x_d = x.rearrange("b (t p) c -> b p t c", p=P)
    adj_d = adj.rearrange("b (t p) j -> b p t j", p=P)
    out_d = out.rearrange("b (t p) c -> b p t c", p=P)
    tables = [nc.dram_tensor(f"feature_table{i}", [N + 1, C], F32, kind="Internal").ap() for i in range(2)]
    table_rows = [table[0:N, :].rearrange("(t p) c -> p t c", p=P) for table in tables]

    with ExitStack() as ctx:
        def sb(name, shape, dt=F32):
            return ctx.enter_context(nc.sbuf_tensor(name, shape, dt))

        def ps(name, shape, dt=F32):
            return ctx.enter_context(nc.psum_tensor(name, shape, dt))

        def sem(name):
            return ctx.enter_context(nc.semaphore(name))

        w0_sb = sb("w0_sb", [P, 2, C])
        b0_sb = sb("b0_sb", [1, C])
        w1_sb = sb("w1_sb", [P, C])
        a1_sb = sb("a1_sb", [P, 2])
        wcat = [sb("wcat1", [P, C + 2]), sb("wcat3", [P, C + 2 * HEADS])]
        src_bc = sb("src_bc", [P, 1 + HEADS, P])
        ww_sb = sb("ww_sb", [P, C])
        qk_w = sb("qk_w", [P, 2, C])
        wb_row = sb("wb_row", [1, C])
        cols = sb("cols", [P, 4])
        a3_sb = sb("a3_sb", [P, 2 * HD])
        ident = sb("ident", [P, P])
        identb = sb("identb", [P, P], BF16)
        ident_big = sb("ident_big", [P, P], BF16)
        ones = sb("ones", [P, P])
        eps_sb = sb("eps_sb", [P, 1])
        pri_i = sb("pri_i", [P, N], mybir.dt.int16)
        zero_row = sb("zero_row", [1, C])

        adj_sb = sb("adj_sb", [P, T, N], I32)
        xin = sb("xin", [P, T, C])
        h0 = sb("h0", [P, T, C])
        h0_t = sb("h0_t", [P, N])
        agg = sb("agg", [P, T, C])
        score = sb("score", [P, N], mybir.dt.float16)
        best_in = sb("best_in", [P, 2, SEGMENTS * 8], mybir.dt.float16)
        vals = sb("vals", [P, 2, TOP])
        flag = sb("flag", [P, 32])
        flag_t = sb("flag_t", [P, 32])
        crowded = sb("crowded", [P, P // 32])
        crowded_any = sb("crowded_any", [1, 1], I32)
        many = sb("many", [P, HALF], I32)
        idx = sb("idx", [P, T, TOP], U32)
        gathered = sb("gathered", [P, RING, SLOTS * C])
        n_st = sb("n_st", [P, T, 6])
        n_mv = sb("n_mv", [P, T, 2])
        n_rstd = sb("n_rstd", [P, T])
        n_shift = sb("n_shift", [P, T])

        x1 = sb("x1", [P, T, C])
        xres = sb("xres", [P, T, C])
        h = sb("h", [P, T, C])
        h_t = sb("h_t", [P, N])
        agg_t = sb("agg_t", [P, N])
        st = sb("st", [P, T, 6])
        mv = sb("mv", [P, T, 2])
        rstd = sb("rstd", [P, T])
        shift = sb("shift", [P, T])
        nmask = sb("nmask", [P, T, N], BF16)
        mask_t = sb("mask_t", [P, T, N], BF16)
        pos = sb("pos", [P, 2, T, N], BF16)
        v_words = T * HEADS * 2 * (HD + 1)
        v_sb = sb("v_sb", [P, v_words])
        vp_sb = sb("vp_sb", [P, 3 * v_words], BF16)
        v = [v_sb[:, 0:T * 2 * (C + 1)].rearrange("p (t h w) -> p t h w", t=T, h=1),
             v_sb[:, :].rearrange("p (t h w) -> p t h w", t=T, h=HEADS)]
        vp = [vp_sb[:, 0:T * 6 * (C + 1)].rearrange("p (t h k w) -> p t h k w", t=T, h=1, k=3),
              vp_sb[:, :].rearrange("p (t h k w) -> p t h k w", t=T, h=HEADS, k=3)]
        dmax = sb("dmax", [HEADS, 1])
        dmax_diag = sb("dmax_diag", [HEADS, HEADS])
        dmax_all = sb("dmax_all", [P, HEADS])
        dist = sb("dist", [P, T, HEADS])
        big_dst = sb("big_dst", [P, T, HEADS])
        reach = sb("reach", [P, T, HEADS])
        beta = sb("beta", [P, T, HEADS])
        o1 = sb("o1", [P, 2, 2 * (C + 1)])
        ww_turned = o1[:, 0, 0:C]
        a3_prod = o1[:, 1, 0:C].rearrange("p (h f) -> p h f", h=HEADS)
        o1_tot = sb("o1_tot", [P, 2, C + 1])
        recip = sb("recip", [P, T, HEADS])
        head_out = v_sb[:, :].rearrange("p (h t w) -> p h t w", h=HEADS, t=T)
        all_out = sb("all_out", [P, T, HEADS, HD + 1])
        pos_f = pos[:, :, :, :].rearrange("p a t n -> p (a t n)").bitcast(F32)
        e_relu = [pos_f[:, i * N:(i + 1) * N] for i in (0, 1)]
        e_sb = [pos_f[:, i * N:(i + 1) * N] for i in (2, 3)]
        p_t = [pos_f[:, i * N:(i + 1) * N] for i in (4, 5)]
        hp = pos_f[:, 7 * N:8 * N].rearrange("p (t c) -> p t c", t=T)
        q_t = v_sb[:, 0:N]
        k_t = v_sb[:, N:2 * N]
        row_max = sb("row_max", [P, T])
        neg_max = sb("neg_max", [P, T])
        row_sum = sb("row_sum", [P, T])
        o2 = sb("o2", [P, 2, C])

        ps_e = ps("ps_e", [P, 4, 512])
        ps_a = ps("ps_a", [P, 2, 512])
        ps_m = ps("ps_m", [P, 512])
        ps_n = ps("ps_n", [P, 512])
        wide_e = [ps_e[:, 2 * i:2 * i + 2, :].rearrange("p b w -> p (b w)") for i in (0, 1)]
        wide_a = ps_a[:, :, :].rearrange("p b w -> p (b w)")
        tiles_a = wide_a.rearrange("p (t w) -> p t w", t=T)
        mask_ps = [ps_e[:, i, :].bitcast(BF16) for i in range(2)]
        wh_banks = [(0, 3, ps_a[:, 0, :]), (3, 6, ps_a[:, 1, :]), (6, 8, ps_m[:, :])]

        GATHER_SIGNALS = 16 * FEW * T // RING
        weights_in = sem("weights_in")
        consts = sem("consts")
        setup_v = sem("setup_v")
        setup_pe = sem("setup_pe")
        x_loaded = sem("x_loaded")
        residual_loaded = sem("residual_loaded")
        requests_begun = sem("requests_begun")
        adj_loaded = [sem(f"adj_loaded{q}") for q in range(4)]
        table_stored = sem("table_stored")
        n_moments = sem("n_moments")
        n_rstd_ready = sem("n_rstd_ready")
        n_shift_ready = sem("n_shift_ready")
        h0_ready = sem("h0_ready")
        h0_turned = sem("h0_turned")
        h0_t_ready = sem("h0_t_ready")
        idx_ready = sem("idx_ready")
        gather_done = [sem(f"gather_done{r}") for r in range(RING)]
        more_done = sem("more_done")
        rest_done = [sem(f"rest_done{r}") for r in range(RING)]
        gathers_begun = sem("gathers_begun")
        agg_ready = sem("agg_ready")
        agg_turned = sem("agg_turned")
        agg_t_ready = sem("agg_t_ready")
        linear_done = sem("linear_done")
        x1_ready = sem("x1_ready")
        v_next = sem("v_next")

        nmask_ready = sem("nmask_ready")
        mask_turned = sem("mask_turned")
        mask_t_ready = sem("mask_t_ready")
        moments = sem("moments")
        act_own = sem("act_own")
        rstd_ready = sem("rstd_ready")
        shift_ready = sem("shift_ready")
        h_ready = sem("h_ready")
        h_turned = sem("h_turned")
        h_t_ready = sem("h_t_ready")
        wh_done = sem("wh_done")
        dst_done = sem("dst_done")
        diag_ready = sem("diag_ready")
        dmax_spread = sem("dmax_spread")
        dist_ready = sem("dist_ready")
        exps_ready = sem("exps_ready")
        v_ready = sem("v_ready")
        part_ready = sem("part_ready")
        rest_ready = sem("rest_ready")
        parts_done = sem("parts_done")
        src_spread = sem("src_spread")
        ramp_ready = sem("ramp_ready")
        pos_ready = sem("pos_ready")
        out1_done = sem("out1_done")
        o1_ready = sem("o1_ready")
        x2_ready = sem("x2_ready")
        qk_done = sem("qk_done")
        qk_ready = sem("qk_ready")
        hp_done = sem("hp_done")
        hp_ready = sem("hp_ready")
        scores_done = sem("scores_done")
        relu_ready = sem("relu_ready")
        masking_begun = sem("masking_begun")
        masked_ready = sem("masked_ready")
        neg_max_ready = sem("neg_max_ready")
        probs_ready = sem("probs_ready")
        probs_turned = sem("probs_turned")
        probs_t_ready = sem("probs_t_ready")
        out2_done = sem("out2_done")
        x3_ready = sem("x3_ready")
        all_done = sem("all_done")
        all_ready = sem("all_ready")
        head_done = sem("head_done")
        head_ready = sem("head_ready")
        x4_ready = sem("x4_ready")
        combined_ready = sem("combined_ready")
        divided = sem("divided")
        stored = sem("stored")
        v_att = sem("v_att")
        v_search = sem("v_search")

        N_WEIGHTS = 14 * 16
        ZERO_ROWS = 2 * 16
        AGG_TURN, AGG_COPY, AGG_LINEAR = (0, 3), (2, 5), (2, 5)
        SUM_AFTER = 5
        NORM_SHIFT = (5, 7)
        PAIR_TOP = (4, 5, 6)
        GROUPS = [[slice(0, 1)], [slice(0, 2), slice(2, HEADS)]]
        GROUP_COUNT = 3

        block = ctx.enter_context(nc.Block())

        @block.sync
        def _(sp):
            loads = [(w0_sb[:, :, :], w0.rearrange("(k p) o -> p k o", p=P)),
                     (b0_sb[:, :], b0.rearrange("(a n) -> a n", a=1)),
                     (w1_sb[:, :], w1), (wcat[0][:, 0:C], w1_t),
                     (a1_sb[:, :], a1),
                     (ww_sb[:, :], ww_t), (qk_w[:, 0, :], qw_t), (qk_w[:, 1, :], kw_t),
                     (wb_row[:, :], wb.rearrange("(a n) -> a n", a=1)),
                     (cols[:, 0:1], wb.rearrange("(p a) -> p a", a=1)),
                     (cols[:, 1:2], qb.rearrange("(p a) -> p a", a=1)),
                     (cols[:, 2:3], kb.rearrange("(p a) -> p a", a=1)),
                     (wcat[1][:, 0:C], w3), (a3_sb[:, :], a3)]

            def load_x(nb):
                sp.dma_start(xin[:, :, :], x_d[nb]).then_inc(x_loaded, 16)

            def load_adj(nb, q):
                sp.dma_start(adj_sb[:, 2 * q:2 * q + 2, :], adj_d[nb, :, 2 * q:2 * q + 2, :])\
                    .then_inc(adj_loaded[q], 16)

            def load_adj_next(nb):
                for q in range(4):
                    sp.wait_ge(nmask_ready, nb * T - T + 2 * q + 2)
                    sp.sem_inc(requests_begun, 1)
                    load_adj(nb, q)

            def load_x_next(nb):
                sp.wait_ge(h0_ready, nb * T)
                sp.sem_inc(requests_begun, 1)
                load_x(nb)

            def load_residual(nb, first):
                if not first:
                    sp.wait_ge(x2_ready, nb * T)
                    sp.sem_inc(requests_begun, 1)
                sp.dma_start(x1[:, :, :], x_d[nb]).then_inc(residual_loaded, 16)

            def store_table(nb, parity, first=False):
                sp.wait_ge(h0_ready, nb * T + T)
                sp.sem_inc(requests_begun, 1)
                if not first:
                    sp.wait_ge(agg_ready, nb * T - T)
                    sp.sem_inc(requests_begun, 1)
                sp.dma_start(table_rows[parity], h0[:, :, :]).then_inc(table_stored, 16)

            def store_out(b):
                sp.wait_ge(x4_ready, b + 1)
                sp.sem_inc(requests_begun, 1)
                sp.dma_start(out_d[b], xres[:, :, :]).then_inc(stored, 16)

            load_x(0)
            for q in range(4):
                load_adj(0, q)
            for dst, src in loads:
                sp.dma_start(dst, src).then_inc(weights_in, 16)
            load_residual(0, True)
            sp.wait_ge(consts, 1)
            for table in tables:
                sp.dma_start(table[N:N + 1, :], zero_row[:, :]).then_inc(stored, 16)
            store_table(0, 0, True)
            load_x_next(1)
            load_adj_next(1)
            store_table(1, 1, True)
            with sp.Fori(0, B - 3, 2) as even:
                for parity in range(2):
                    b = even + parity
                    load_x_next(b + 2)
                    load_residual(b + 1, False)
                    load_adj_next(b + 2)
                    store_table(b + 2, parity)
                    store_out(b)
            load_residual(B - 1, False)
            store_out(B - 2)
            store_out(B - 1)
            sp.wait_ge(stored, ZERO_ROWS + B * 16)

        @block.gpsimd
        def _(pool):
            pool.memset(zero_row[:, :], 0.0).then_inc(consts, 1)
            pool.memset(ident[:, :], 0.0).then_inc(consts, 1)
            pool.memset(ones[:, :], 1.0).then_inc(consts, 1)
            pool.memset(flag[:, :], 0.0).then_inc(consts, 1)
            pool.memset(eps_sb[:, :], EPS).then_inc(consts, 1)
            pool.iota(pri_i[:, :], [[-1, N]], base=N, channel_multiplier=0).then_inc(consts, 1)
            pool.wait_ge(consts, 6)
            pool.affine_select(out=ident[:, :], in_=ident[:, :], compare_op=ALU.not_equal, fill=1.0,
                               base=0, pattern=[[-1, P]], channel_multiplier=1).then_inc(consts, 1)

            def finish(b):
                pool.wait_ge(combined_ready, b + 1)
                pool.sem_inc(gathers_begun, 1)
                res = xres[:, :, :].rearrange("p t (h f) -> p t h f", h=HEADS)
                n = all_out[:, :, :, 0:HD]
                pool.tensor_tensor(n, n, recip[:, :, :].unsqueeze(3).broadcast_to([P, T, HEADS, HD]), ALU.mult)\
                    .then_inc(divided, 1)
                pool.wait_ge(divided, b + 1)
                pool.tensor_tensor(res, n, res, ALU.add).then_inc(x4_ready, 1)

            def gathers(nb, parity, first, finishing):
                pool.wait_ge(table_stored, nb * 16 + 16)
                for t in range(T):
                    pool.wait_ge(idx_ready, nb * HALF + t // 2 + 1)
                    if not (first and t < RING):
                        pool.wait_ge(agg_ready, nb * T + t + 1 - RING)
                    pool.sem_inc(gathers_begun, 1)

                    def gather(slots, done):
                        for s in slots:
                            pool.indirect_dma_start(
                                out=gathered[:, t % RING, s * C:(s + 1) * C], out_offset=None, in_=tables[parity],
                                in_offset=bass.IndirectOffsetOnAxis(ap=idx[:, t, s:s + 1], axis=0),
                            ).then_inc(done, 16)

                    gather(range(FEW), gather_done[t % RING])
                    if t == 0 and finishing:
                        finish(nb - 2)
                    more = sum(pool.value_load(many[k + t % 2:k + t % 2 + 1, t // 2:t // 2 + 1], min_val=0, max_val=N)
                               for k in range(0, P, 32))
                    with pool.If(more > 0):
                        gather(range(FEW, SLOTS), more_done)
                        pool.reg_add(more_count, more_count, 16 * (SLOTS - FEW))
                        pool.wait_ge(more_done, more_count)
                        pool.sem_inc(rest_done[t % RING], 1)
                    with pool.Else():
                        pool.memset(gathered[:, t % RING, FEW * C:SLOTS * C], 0.0)\
                            .then_inc(rest_done[t % RING], 1)

            pool.wait_ge(stored, ZERO_ROWS)
            more_count = pool.alloc_register("more_count")
            pool.reg_mov(more_count, 0)
            gathers(0, 0, True, False)
            gathers(1, 1, False, False)
            with pool.Fori(0, B - 3, 2) as even:
                for parity in range(2):
                    gathers(even + 2 + parity, parity, False, True)
            finish(B - 2)
            finish(B - 1)

        @block.scalar
        def _(act):
            act.preload_act_table_set("natural_log_exp_and_others")

            def deviation(mv_, rstd_, f, at, mom, rr):
                half = slice(HALF * f, HALF * f + HALF)
                act.wait_ge(mom, at + f + 1)
                act.activation(rstd_[:, half], mv_[:, half, 1], ACT.Ln, bias=eps_sb[:, 0:1])\
                    .then_inc(act_own, own.one())
                act.wait_ge(act_own, own.value)
                act.activation(rstd_[:, half], rstd_[:, half], ACT.Exp, scale=-0.5).then_inc(rr, 1)

            def normalise(src, dst, rstd_, shift_, f, at, rr, sr, ready):
                act.wait_ge(rr, at + f + 1)
                act.wait_ge(sr, at + f + 1)
                for t in range(HALF * f, HALF * f + HALF):
                    act.activation(dst[:, t, :], src[:, t, :], ACT.Relu, bias=shift_[:, t:t + 1],
                                   scale=rstd_[:, t:t + 1]).then_inc(ready, 1)

            def next_deviation(nb, f):
                deviation(n_mv, n_rstd, f, nb * 2, n_moments, n_rstd_ready)

            def next_norm(nb, f, first):
                if not first:
                    act.wait_ge(table_stored, nb * 16)
                normalise(xin, h0, n_rstd, n_shift, f, nb * 2, n_rstd_ready, n_shift_ready, h0_ready)

            def next_turn_features(nb):
                for f in range(2):
                    act.wait_ge(h0_turned, nb * 2 + f + 1)
                    act.activation(h0_t[:, f * 512:f * 512 + 512], (ps_n, ps_m)[f][:, :], ACT.Copy)\
                        .then_inc(h0_t_ready, 1)

            def next_turn(nb, f):
                act.wait_ge(agg_turned, nb * 2 + f + 1)
                act.activation(agg_t[:, f * 512:f * 512 + 512], ps_n[:, :], ACT.Copy)\
                    .then_inc(agg_t_ready, 1)

            def layer_deviation(b, layer, f):
                deviation(mv, rstd, f, b * 6 + 2 * layer, moments, rstd_ready)

            def layer_norm(b, layer, f):
                normalise(xres if layer else x1, h, rstd, shift, f, b * 6 + 2 * layer, rstd_ready, shift_ready,
                          h_ready)

            def turn(b, layer, f):
                act.wait_ge(h_turned, b * 6 + 2 * layer + f + 1)
                act.activation(h_t[:, f * 512:f * 512 + 512], ps_a[:, f, :] if layer == 2 else (ps_n, ps_m)[f][:, :],
                               ACT.Copy).then_inc(h_t_ready, 1)

            def exps(b, g):
                H, Fd = GAT[g]
                act.wait_ge(dist_ready, b * 2 + g + 1)
                act.activation(v[g][:, :, :, Fd], dist[:, :, 0:H], ACT.Exp)
                act.activation(v[g][:, :, :, 2 * Fd + 1], dist[:, :, 0:H], ACT.Exp, scale=SLOPE)
                act.activation(beta[:, :, 0:H], reach[:, :, 0:H], ACT.Relu).then_inc(act_own, own.one())
                act.wait_ge(act_own, own.value)
                act.activation(beta[:, :, 0:H], beta[:, :, 0:H], ACT.Exp, scale=SLOPE - 1.0)\
                    .then_inc(exps_ready, 1)

            def split(b, g, group, k):
                hs = GROUPS[g][group]
                if k == 0:
                    act.wait_ge(v_ready, b * GROUP_COUNT + g + group + 1)
                else:
                    act.wait_ge(rest_ready, b * GROUP_COUNT + g + group + 1)
                act.activation(vp[g][:, :, hs, k, :], v[g][:, :, hs, :], ACT.Copy).then_inc(part_ready, 1)

            def ramps(b, g, head, js):
                k = head if g == 0 else 1 + head
                act.wait_ge(src_spread, b * (1 + HEADS) + k + 1)
                if g and head >= 2:
                    act.wait_ge(head_done, b * HEADS + head - 1)
                for j in js:
                    act.activation(pos[:, head % 2, j, :], wide_e[head % 2 if g else 1], ACT.Relu,
                                   bias=big_dst[:, j, head:head + 1], scale=STEEP).then_inc(ramp_ready, 1)

            def turn_mask(b, j):
                act.wait_ge(mask_turned, b * T + j + 1)
                act.activation(mask_t[:, j, :], mask_ps[j % 2], ACT.Identity, bias=ones[:, 0:1])\
                    .then_inc(mask_t_ready, 1)

            def attention(b, has_next, has_far):
                nonlocal own
                own = Own()
                for j in (0, 1):
                    turn_mask(b, j)
                exps(b, 0)
                ramps(b, 0, 0, (0, 1))
                for j in (2,):
                    turn_mask(b, j)
                split(b, 0, 0, 0)
                for j in (3, 4):
                    turn_mask(b, j)
                split(b, 0, 0, 1)
                for j in (5, 6, 7):
                    turn_mask(b, j)
                ramps(b, 0, 0, range(2, T))
                if has_next:
                    next_turn_features(b + 1)
                for t in range(T):
                    act.wait_ge(out1_done, b * T + t + 1)
                    if t >= 2:
                        act.wait_ge(x2_ready, b * T + t - 1)
                    act.activation(o1[:, t % 2, :], ps_a[:, t % 2, 0:2 * (C + 1)], ACT.Copy)\
                        .then_inc(o1_ready, 1)
                    if t == 5:
                        layer_deviation(b, 1, 0)
                    if t == 6:
                        layer_norm(b, 1, 0)
                layer_deviation(b, 1, 1)
                turn(b, 1, 0)
                layer_norm(b, 1, 1)
                turn(b, 1, 1)
                act.wait_ge(qk_done, b * 2 + 1)
                act.activation(q_t, wide_e[0], ACT.Identity, bias=cols[:, 3:4], scale=SLOPE * SCORE_SCALE)\
                    .then_inc(qk_ready, 1)
                act.wait_ge(qk_done, b * 2 + 2)
                act.activation(k_t, wide_e[1], ACT.Identity, bias=cols[:, 2:3]).then_inc(qk_ready, 1)
                act.wait_ge(hp_done, b + 1)
                act.activation(hp, tiles_a, ACT.Copy).then_inc(hp_ready, 1)
                for t in range(T + 1):
                    if t:
                        act.wait_ge(neg_max_ready, b * T + t)
                        act.activation(e_sb[(t - 1) % 2], e_sb[(t - 1) % 2], ACT.Exp, bias=neg_max[:, t - 1:t],
                                       accum_out=row_sum[:, t - 1:t]).then_inc(probs_ready, 1)
                    if t < T:
                        act.wait_ge(scores_done, b * T + t + 1)
                        if t >= 2:
                            act.wait_ge(masked_ready, b * T + t - 1)
                        act.activation(e_relu[t % 2], wide_e[t % 2], ACT.Relu, scale=(1.0 - SLOPE) / SLOPE)\
                            .then_inc(relu_ready, 1)
                    if t:
                        act.wait_ge(probs_turned, b * T + t)
                        if t > 2:
                            act.wait_ge(out2_done, b * T + t - 2)
                        act.activation(p_t[(t - 1) % 2], wide_a, ACT.Copy).then_inc(probs_t_ready, 1)
                    if has_far and t == 4:
                        for f in range(2):
                            next_deviation(b + 2, f)
                    if has_far and t in (6, 7):
                        next_norm(b + 2, t - 6, False)
                    if t == 6:
                        layer_deviation(b, 2, 0)
                    if t == T:
                        layer_norm(b, 2, 0)
                layer_deviation(b, 2, 1)
                turn(b, 2, 0)
                layer_norm(b, 2, 1)
                turn(b, 2, 1)
                exps(b, 1)
                ramps(b, 1, 0, range(0, 2))
                split(b, 1, 0, 0)
                ramps(b, 1, 0, range(2, 3))
                split(b, 1, 0, 1)
                ramps(b, 1, 0, range(3, T))
                split(b, 1, 1, 0)
                ramps(b, 1, 1, range(0, 3))
                split(b, 1, 1, 1)
                for head in range(1, HEADS):
                    ramps(b, 1, head, range(0 if head > 1 else 3, T))
                    if has_next and head in AGG_COPY:
                        next_turn(b + 1, AGG_COPY.index(head))
                    if has_next and head - 2 in AGG_LINEAR:
                        layer_deviation(b + 1, 0, AGG_LINEAR.index(head - 2))
                    if has_next and head == HEADS - 2:
                        layer_norm(b + 1, 0, 0)
                if has_next:
                    layer_norm(b + 1, 0, 1)
                    for f in range(2):
                        turn(b + 1, 0, f)
                act.wait_ge(act_own, own.value)
                act.sem_clear(act_own)

            own = Own()
            act.wait_ge(consts, 7)
            act.wait_ge(weights_in, N_WEIGHTS)
            for f in range(2):
                next_deviation(0, f)
                next_norm(0, f, True)
            next_turn_features(0)
            for f in range(2):
                next_deviation(1, f)
                next_norm(1, f, False)
            for f in range(2):
                next_turn(0, f)
                layer_deviation(0, 0, f)
                layer_norm(0, 0, f)
            for f in range(2):
                turn(0, 0, f)
            act.wait_ge(act_own, own.value)
            act.sem_clear(act_own)
            with act.Fori(0, B - 2) as b:
                attention(b, True, True)
            attention(B - 2, True, False)
            attention(B - 1, False, False)

        @block.tensor
        def _(pe):
            def rows(t):
                return slice(t * P, t * P + P)

            def next_turn_features(nb, first):
                if not first:
                    pe.wait_ge(v_ready, (nb - 1) * GROUP_COUNT + 1)
                for f in range(2):
                    pe.wait_ge(h0_ready, nb * T + HALF * (f + 1))
                    for t in range(HALF):
                        last = pe.transpose((ps_n, ps_m)[f][:, rows(t)], h0[:, HALF * f + t, :], ident[:, :])
                    last.then_inc(h0_turned, 1)

            def next_turn(nb, f):
                pe.wait_ge(agg_ready, nb * T + HALF * (f + 1))
                if f:
                    pe.wait_ge(x1_ready, nb * 2 + 1)
                for t in range(HALF):
                    last = pe.transpose(ps_n[:, rows(t)], agg[:, HALF * f + t, :], ident[:, :])
                last.then_inc(agg_turned, 1)

            def next_linear(nb, f):
                pe.wait_ge(h0_t_ready, nb * 2 + 2)
                pe.wait_ge(agg_t_ready, nb * 2 + f + 1)
                for t in range(HALF):
                    o, tile = ps_n[:, rows(t)], rows(HALF * f + t)
                    pe.matmul(o, h0_t[:, tile], w0_sb[:, 0, :], start=True, stop=False)
                    pe.matmul(o, agg_t[:, tile], w0_sb[:, 1, :], start=False, stop=False)
                    last = pe.matmul(o, ones[0:1, :], b0_sb[:, :], start=False, stop=True)
                last.then_inc(linear_done, 1)

            def turn(b, layer):
                for f in range(2):
                    pe.wait_ge(h_ready, b * 3 * T + T * layer + HALF * (f + 1))
                    o = ps_a[:, f, :] if layer == 2 else (ps_n, ps_m)[f][:, :]
                    for t in range(HALF):
                        last = pe.transpose(o[:, rows(t)], h[:, HALF * f + t, :], ident[:, :])
                    last.then_inc(h_turned, 1)

            def wide(o, lhs, rhs):
                for f in range(2):
                    last = pe.matmul(o[:, f * 512:f * 512 + 512], lhs, rhs[:, f * 512:f * 512 + 512],
                                     start=True, stop=True)
                return last

            def project(b, g):
                H, Fd = GAT[g]
                pe.wait_ge(h_t_ready, b * 6 + 4 * g + 2)
                wide(wide_e[1][0:H, :], wcat[g][:, C + H:C + 2 * H], h_t).then_inc(dst_done, 1)
                for t0, t1, bank in wh_banks:
                    for t in range(t0, t1):
                        o = bank[:, (t - t0) * WH:(t - t0) * WH + C + 2 * H]
                        last = pe.matmul(o, h_t[:, rows(t)], wcat[g][:, 0:C + 2 * H], start=True, stop=True)
                last.then_inc(wh_done, 1)

            def spread_max(b, g):
                H, Fd = GAT[g]
                pe.wait_ge(diag_ready, b * 2 + g + 1)
                pe.matmul(ps_n[:, 0:H], ones[0:H, :], dmax_diag[0:H, 0:H], start=True, stop=True)\
                    .then_inc(dmax_spread, 1)

            def spread_source(b, g, head):
                k = head if g == 0 else 1 + head
                if head >= 2:
                    pe.wait_ge(pos_ready, b * T * (1 + HEADS) + T * k - T)
                wide(wide_e[head % 2 if g else 1], src_bc[:, k, :], h_t).then_inc(src_spread, 1)

            def turn_mask(b, j):
                if j >= 2:
                    pe.wait_ge(mask_t_ready, b * T + j - 1)
                for t in range(T):
                    if j == 0:
                        pe.wait_ge(nmask_ready, b * T + t + 1)
                    last = pe.transpose(mask_ps[j % 2][:, rows(t)], nmask[:, t, rows(j)], identb[:, :])
                last.then_inc(mask_turned, 1)

            def attention(b, has_next, has_far):
                project(b, 0)
                for j in (0, 1):
                    turn_mask(b, j)
                spread_max(b, 0)
                spread_source(b, 0, 0)
                for j in range(2, T):
                    turn_mask(b, j)
                if has_next:
                    next_turn_features(b + 1, False)
                pe.wait_ge(parts_done, b * GROUP_COUNT + 1)
                W = C + 1
                for t in range(T):
                    if t >= 2:
                        pe.wait_ge(o1_ready, b * T + t - 1)
                    for part in range(2):
                        o = ps_a[:, t % 2, part * W:part * W + W]
                        for n in range(3 * T):
                            j, k = n // 3, n % 3
                            if t == 0 and part == 0 and k == 0:
                                pe.wait_ge(pos_ready, b * T * (1 + HEADS) + j + 1)
                            last = pe.matmul(o, pos[:, part, j, rows(t)], vp[0][:, j, 0, k, part * W:part * W + W],
                                             start=(n == 0), stop=(n == 3 * T - 1))
                    last.then_inc(out1_done, 1)
                turn(b, 1)
                pe.wait_ge(h_t_ready, b * 6 + 4)
                wide(wide_e[0], qk_w[:, 0, :], h_t).then_inc(qk_done, 1)
                wide(wide_e[1], qk_w[:, 1, :], h_t).then_inc(qk_done, 1)
                for t in range(T):
                    pe.matmul(tiles_a[:, t, :], h_t[:, rows(t)], ww_sb[:, :], start=True, stop=False)
                    last = pe.matmul(tiles_a[:, t, :], ones[0:1, :], wb_row[:, :], start=False, stop=True)
                last.then_inc(hp_done, 1)
                pe.wait_ge(qk_ready, b * 2 + 2)
                for t in range(T + 2):
                    if t < T:
                        if t >= 2:
                            pe.wait_ge(masked_ready, b * T + t - 1)
                        for f in range(2):
                            o, c = wide_e[t % 2][:, f * 512:f * 512 + 512], slice(f * 512, f * 512 + 512)
                            pe.matmul(o, q_t[:, rows(t)], k_t[:, c], start=True, stop=False)
                            last = pe.matmul(o, ident_big[:, :], nmask[:, t, c], start=False, stop=True)
                        last.then_inc(scores_done, 1)
                    if 1 <= t <= T:
                        u = t - 1
                        pe.wait_ge(probs_ready, b * T + u + 1)
                        if u == 0:
                            pe.wait_ge(hp_ready, b + 1)
                        else:
                            pe.wait_ge(probs_t_ready, b * T + u)
                        for j in range(T):
                            last = pe.transpose(tiles_a[:, j, :], e_sb[u % 2][:, rows(j)], ident[:, :])
                        last.then_inc(probs_turned, 1)
                    if t >= 2:
                        u = t - 2
                        pe.wait_ge(probs_t_ready, b * T + u + 1)
                        if u >= 2:
                            pe.wait_ge(x3_ready, b * T + u - 1)
                        elif u == 0 and has_next:
                            pe.wait_ge(h0_t_ready, (b + 1) * 2 + 2)
                        for j in range(T):
                            last = pe.matmul((ps_m, ps_n)[u % 2][:, 0:C], p_t[u % 2][:, rows(j)], hp[:, j, :],
                                             start=(j == 0), stop=(j == T - 1))
                        last.then_inc(out2_done, 1)
                turn(b, 2)
                project(b, 1)
                spread_source(b, 1, 0)
                spread_max(b, 1)
                spread_source(b, 1, 1)
                pe.wait_ge(parts_done, b * GROUP_COUNT + 2)
                pe.wait_ge(v_ready, b * GROUP_COUNT + 3)
                W = HD + 1
                for head in range(HEADS):
                    if head:
                        pe.wait_ge(head_ready, b * HEADS + head)
                    for t in range(T):
                        for j in range(T):
                            if t == 0:
                                pe.wait_ge(pos_ready, b * T * (1 + HEADS) + T * (1 + head) + j + 1)
                            last = pe.matmul(tiles_a[:, t, 0:6 * W], pos[:, head % 2, j, rows(t)],
                                             vp[1][:, j, head, :, :].rearrange("p k w -> p (k w)"),
                                             start=(j == 0), stop=(j == T - 1))
                    last.then_inc(head_done, 1)
                    if head + 2 < HEADS:
                        spread_source(b, 1, head + 2)
                    if head == 0:
                        pe.wait_ge(parts_done, b * GROUP_COUNT + 3)
                    else:
                        pe.wait_ge(all_ready, b * T + head)
                    for j in range(T):
                        last = pe.matmul(ps_m[:, 0:3 * HEADS * W], mask_t[:, j, rows(head)],
                                         vp[1][:, j, :, :, W:2 * W].rearrange("p h k w -> p (h k) w"),
                                         start=(j == 0), stop=(j == T - 1))
                    last.then_inc(all_done, 1)
                    if has_next and head in AGG_LINEAR:
                        next_linear(b + 1, AGG_LINEAR.index(head))
                    if has_next and head in AGG_TURN:
                        next_turn(b + 1, AGG_TURN.index(head))
                if has_next:
                    pe.wait_ge(all_ready, b * T + T)
                    pe.wait_ge(head_ready, b * HEADS + HEADS)
                    pe.wait_ge(x1_ready, b * 2 + 4)
                    turn(b + 1, 0)

            pe.wait_ge(consts, 7)
            pe.wait_ge(weights_in, N_WEIGHTS)
            pe.matmul(ps_e[:, 3, 0:2], w1_sb[:, :], a1_sb[:, :], start=True, stop=True).then_inc(setup_pe, 1)
            pe.transpose(ps_e[:, 2, 0:C], ww_sb[:, :], ident[:, :]).then_inc(setup_pe, 1)
            pe.wait_ge(setup_v, 9)
            for i in range(2):
                pe.matmul(ps_e[:, 1, i * C:i * C + C], ww_turned, qk_w[:, i, :], start=True, stop=True)
                last = pe.matmul(ps_e[:, 1, 2 * C + i:2 * C + i + 1], qk_w[:, i, :], cols[:, 0:1],
                                 start=True, stop=True)
            last.then_inc(setup_pe, 1)
            next_turn_features(0, True)
            for f in range(2):
                if f == 0:
                    pe.wait_ge(h0_t_ready, 2)
                next_turn(0, f)
                next_linear(0, f)
            pe.wait_ge(x1_ready, 2)
            turn(0, 0)
            pe.wait_ge(setup_v, 11)
            with pe.Fori(0, B - 2) as b:
                attention(b, True, True)
            attention(B - 2, True, False)
            attention(B - 1, False, False)

        @block.vector
        def _(dve):
            def moments_of(src, st_, mv_, f, own_sem, own, mom):
                tiles = range(HALF * f, HALF * f + HALF)
                for t in tiles:
                    dve.bn_stats(st_[:, t, :], src[:, t, :]).then_inc(own_sem, own.one())
                dve.wait_ge(own_sem, own.value)
                for t in tiles:
                    last = dve.bn_aggr(mv_[:, t, :], st_[:, t, :])
                last.then_inc(mom, 1)

            def shift_of(mv_, rstd_, shift_, f, at, rr, sr):
                half = slice(HALF * f, HALF * f + HALF)
                dve.wait_ge(rr, at + f + 1)
                dve.scalar_tensor_tensor(out=shift_[:, half], in0=mv_[:, half, 0], scalar=-1.0, in1=rstd_[:, half],
                                         op0=ALU.mult, op1=ALU.mult).then_inc(sr, 1)

            def layer_moments(b, layer, f):
                dve.wait_ge(x3_ready if layer == 2 else x2_ready, b * T + HALF * f + HALF)
                moments_of(xres, st, mv, f, v_att, ch, moments)

            def layer_shift(b, layer, f):
                shift_of(mv, rstd, shift, f, b * 6 + 2 * layer, rstd_ready, shift_ready)

            def score_of(t):
                return dve.scalar_tensor_tensor(out=score[:, :], in0=adj_sb[:, t, :], scalar=0.0, in1=pri_i[:, :],
                                                op0=ALU.not_equal, op1=ALU.mult)

            def segment_tops(nb, own, q, i):
                if own.value:
                    dve.wait_ge(v_next, own.value)
                if i == 0:
                    dve.wait_ge(adj_loaded[q], nb * 16 + 16)
                score_of(2 * q + i).then_inc(v_next, own.one())
                dve.wait_ge(v_next, own.value)
                for g in range(SEGMENTS):
                    width = N // SEGMENTS
                    last = dve.max(best_in[:, i, 8 * g:8 * g + 8], score[:, width * g:width * g + width])
                last.then_inc(v_next, own.one())

            def over_rows(own, out):
                dve.wait_ge(v_next, own.value)
                dve.transpose(flag_t[:, :], flag[:, :]).then_inc(v_next, own.one())
                dve.wait_ge(v_next, own.value)
                dve.tensor_reduce(out, flag_t[:, :], AX.X, ALU.max).then_inc(v_next, own.one())

            def settle_crowds(own, q):
                dve.wait_ge(v_next, own.value)
                dve.tensor_reduce(flag[:, 0:1], best_in[:, :, 7:SEGMENTS * 8:8], AX.XY, ALU.max)\
                    .then_inc(v_next, own.one())
                over_rows(own, crowded[:, 0:1])
                dve.wait_ge(v_next, own.value)
                for k in range(1, P // 32):
                    last = dve.tensor_copy(crowded[0:1, k:k + 1], crowded[32 * k:32 * k + 1, 0:1])
                last.then_inc(v_next, own.one())
                dve.wait_ge(v_next, own.value)
                dve.tensor_reduce(crowded_any[0:1, :], crowded[0:1, :], AX.X, ALU.max).then_inc(v_next, own.one())
                dve.wait_ge(v_next, own.value)
                crowds = dve.value_load(crowded_any[0:1, 0:1], min_val=0, max_val=N)
                with dve.If(crowds > 0):
                    searched = Own()
                    for i in range(2):
                        score_of(2 * q + i).then_inc(v_search, searched.one())
                        dve.memset(best_in[:, i, TOP:], 0.0)
                        dve.wait_ge(v_search, searched.value)
                        for r in range(TOP // 8):
                            best = best_in[:, i, 8 * r:8 * r + 8]
                            dve.max(best, score[:, :]).then_inc(v_search, searched.one())
                            dve.wait_ge(v_search, searched.value)
                            if r < TOP // 8 - 1:
                                dve.tensor_copy(vals[:, i, 8 * r:8 * r + 8], best).then_inc(v_search, searched.one())
                                dve.wait_ge(v_search, searched.value)
                                dve.match_replace(score[:, :], vals[:, i, 8 * r:8 * r + 8], score[:, :], 0.0)\
                                    .then_inc(v_search, searched.one())
                                dve.wait_ge(v_search, searched.value)
                    dve.sem_clear(v_search)

            def tops(own, q):
                for r in range(TOP // 8):
                    for i in range(2):
                        if r:
                            dve.wait_ge(v_next, own.value - 1)
                        dve.max(vals[:, i, 8 * r:8 * r + 8], best_in[:, i, :]).then_inc(v_next, own.one())
                    if r < TOP // 8 - 1:
                        for i in range(2):
                            dve.wait_ge(v_next, own.value - 1)
                            dve.match_replace(best_in[:, i, :], vals[:, i, 8 * r:8 * r + 8], best_in[:, i, :], 0.0)\
                                .then_inc(v_next, own.one())
                dve.wait_ge(v_next, own.value)
                dve.tensor_scalar(idx[:, 2 * q:2 * q + 2, :], vals[:, :, :], -1.0, float(N), ALU.mult, ALU.add)
                dve.tensor_copy(flag[:, 0:2], vals[:, :, FEW]).then_inc(v_next, own.one())
                over_rows(own, many[:, q:q + 1])
                dve.wait_ge(v_next, own.value)
                dve.sem_inc(idx_ready, 1)

            def top(nb, own, q, part):
                if part < 2:
                    segment_tops(nb, own, q, part)
                if part == 1:
                    settle_crowds(own, q)
                if part == 2:
                    tops(own, q)

            def reduce(nb, t):
                dve.wait_ge(gather_done[t % RING], nb * GATHER_SIGNALS + 16 * FEW * (t // RING + 1))
                dve.wait_ge(rest_done[t % RING], nb * (T // RING) + t // RING + 1)
                dve.tensor_reduce(agg[:, t, :], gathered[:, t % RING, :].rearrange("p (s c) -> p c s", s=SLOTS),
                                  AX.X, ALU.max).then_inc(agg_ready, 1)

            def next_finish(nb, f):
                dve.wait_ge(linear_done, nb * 2 + f + 1)
                dve.wait_ge(residual_loaded, nb * 16 + 16)
                s = slice(HALF * f, HALF * f + HALF)
                dve.scalar_tensor_tensor(out=x1[:, s, :], in0=ps_n[:, :].rearrange("p (t c) -> p t c", c=C),
                                         scalar=0.0, in1=x1[:, s, :], op0=ALU.max, op1=ALU.add)\
                    .then_inc(x1_ready, 1)

            def spread_max(b, g):
                H, Fd = GAT[g]
                dve.wait_ge(dst_done, b * 2 + g + 1)
                dve.tensor_reduce(dmax[0:H, :], wide_e[1][0:H, :], AX.X, ALU.max).then_inc(v_att, ch.one())
                dve.wait_ge(v_att, ch.value)
                dve.tensor_scalar(dmax_diag[0:H, 0:H], ident[0:H, 0:H], dmax[0:H, 0:1], None, ALU.mult)\
                    .then_inc(diag_ready, 1)

            def distances(b, g):
                H, Fd = GAT[g]
                dve.wait_ge(dmax_spread, b * 2 + g + 1)
                dve.tensor_copy(dmax_all[:, 0:H], ps_n[:, 0:H]).then_inc(v_att, ch.one())
                dve.wait_ge(v_att, ch.value)
                dve.wait_ge(wh_done, b * 2 + g + 1)
                for t0, t1, bank in wh_banks:
                    node = bank[:, 0:(t1 - t0) * WH].rearrange("p (t w) -> p t w", w=WH)
                    src, dst = node[:, :, C:C + H], node[:, :, C + H:C + 2 * H]
                    top_d = dmax_all[:, 0:H].unsqueeze(1).broadcast_to([P, t1 - t0, H])
                    dve.tensor_tensor(reach[:, t0:t1, 0:H], src, top_d, ALU.add)
                    dve.tensor_scalar(big_dst[:, t0:t1, 0:H], dst, STEEP, None, ALU.mult)
                    last = dve.tensor_tensor(dist[:, t0:t1, 0:H], dst, top_d, ALU.subtract)
                last.then_inc(dist_ready, 1)

            def scaled_values(b, g, group):
                H, Fd = GAT[g]
                hs = GROUPS[g][group]
                count = hs.stop - hs.start
                dve.wait_ge(exps_ready, b * 2 + g + 1)
                for t0, t1, bank in wh_banks:
                    wh = bank[:, 0:(t1 - t0) * WH].rearrange("p (t w) -> p t w", w=WH)[:, :, hs.start * Fd:hs.stop * Fd]
                    for half in range(2):
                        at = half * (Fd + 1)
                        vt = v[g][:, t0:t1, hs, :]
                        if H == 1:
                            e = vt[:, :, 0, at + Fd:at + Fd + 1].broadcast_to([P, t1 - t0, Fd])
                            last = dve.tensor_tensor(vt[:, :, 0, at:at + Fd], wh, e, ALU.mult)
                        else:
                            e = vt[:, :, :, at + Fd:at + Fd + 1].broadcast_to([P, t1 - t0, count, Fd])
                            last = dve.tensor_tensor(vt[:, :, :, at:at + Fd],
                                                     wh.rearrange("p t (h f) -> p t h f", h=count), e, ALU.mult)
                last.then_inc(v_ready, 1)

            def split(b, g, group):
                hs = GROUPS[g][group]
                dve.wait_ge(part_ready, (b * GROUP_COUNT + g + group) * 2 + 1)
                dve.wait_ge(v_ready, b * GROUP_COUNT + g + group + 1)
                rest = v[g][:, :, hs, :]
                dve.tensor_tensor(rest, rest, vp[g][:, :, hs, 0, :], ALU.subtract).then_inc(rest_ready, 1)

            def split_last(b, g, group):
                hs = GROUPS[g][group]
                dve.wait_ge(part_ready, (b * GROUP_COUNT + g + group) * 2 + 2)
                dve.tensor_tensor(vp[g][:, :, hs, 2, :], v[g][:, :, hs, :], vp[g][:, :, hs, 1, :], ALU.subtract)\
                    .then_inc(parts_done, 1)

            def positive(b, head, j):
                dve.wait_ge(ramp_ready, b * T * (1 + HEADS) + (1 + head) * T + j + 1)
                here = pos[:, head % 2, j, :]
                dve.tensor_tensor(here, here, mask_t[:, j, :], ALU.min).then_inc(pos_ready, 1)

            def positive_and_other(b, j):
                for i in (j, j + 1):
                    dve.wait_ge(ramp_ready, b * T * (1 + HEADS) + i + 1)
                    here = pos[:, 0, i, :]
                    dve.tensor_tensor(here, here, mask_t[:, i, :], ALU.min).then_inc(v_att, ch.one())
                for i in (j, j + 1):
                    dve.wait_ge(v_att, ch.value - (j + 1 - i))
                    dve.tensor_tensor(pos[:, 1, i, :], mask_t[:, i, :], pos[:, 0, i, :], ALU.subtract)\
                        .then_inc(pos_ready, 1)

            def combine1(b, t):
                W = C + 1
                dve.wait_ge(o1_ready, b * T + t + 1)
                if t == 0:
                    dve.wait_ge(stored, ZERO_ROWS + b * 16)
                o, tot = o1[:, t % 2, :], o1_tot[:, t % 2, :]
                dve.scalar_tensor_tensor(out=tot, in0=o[:, W:2 * W], scalar=beta[:, t, 0:1], in1=o[:, 0:W],
                                         op0=ALU.mult, op1=ALU.add).then_inc(v_att, ch.one())
                dve.wait_ge(v_att, ch.value)
                dve.reciprocal(recip[:, t, 0:1], tot[:, C:W]).then_inc(v_att, ch.one())
                dve.wait_ge(v_att, ch.value)
                dve.scalar_tensor_tensor(out=xres[:, t, :], in0=tot[:, 0:C], scalar=recip[:, t, 0:1],
                                         in1=x1[:, t, :], op0=ALU.mult, op1=ALU.add).then_inc(x2_ready, 1)

            def masked_max(b, t):
                dve.wait_ge(relu_ready, b * T + t + 1)
                if t >= 2:
                    dve.wait_ge(probs_turned, b * T + t - 1)
                dve.sem_inc(masking_begun, 1)
                dve.tensor_tensor_reduce(out=e_sb[t % 2], in0=wide_e[t % 2], in1=e_relu[t % 2], scale=1.0,
                                         scalar=-3.0e38, op0=ALU.add, op1=ALU.max,
                                         accum_out=row_max[:, t:t + 1]).then_inc(masked_ready, 1)
                dve.wait_ge(masked_ready, b * T + t + 1)
                dve.tensor_scalar(neg_max[:, t:t + 1], row_max[:, t:t + 1], -1.0, None, ALU.mult)\
                    .then_inc(neg_max_ready, 1)

            def combine2(b, t):
                dve.wait_ge(out2_done, b * T + t + 1)
                dve.reciprocal(recip[:, t, 0:1], row_sum[:, t:t + 1]).then_inc(v_att, ch.one())
                dve.wait_ge(v_att, ch.value)
                dve.tensor_scalar(o2[:, t % 2, :], (ps_m, ps_n)[t % 2][:, 0:C], 0.0,
                                          recip[:, t, 0:1], ALU.max, ALU.mult).then_inc(v_att, ch.one())
                dve.wait_ge(v_att, ch.value)
                dve.tensor_tensor(xres[:, t, :], xres[:, t, :], o2[:, t % 2, :], ALU.add)\
                    .then_inc(x3_ready, 1)

            def sum_all(b, t):
                dve.wait_ge(all_done, b * T + t + 1)
                W = HD + 1
                dve.tensor_reduce(all_out[:, t, :, :],
                                          ps_m[:, 0:3 * HEADS * W].rearrange("p (h k w) -> p h w k", h=HEADS, k=3),
                                          AX.X, ALU.add).then_inc(all_ready, 1)

            def sum_head(b, head):
                if head == 0:
                    dve.wait_ge(parts_done, b * GROUP_COUNT + 3)
                dve.wait_ge(head_done, b * HEADS + head + 1)
                W = 2 * (HD + 1)
                dve.tensor_reduce(head_out[:, head, :, :],
                                  tiles_a[:, :, 0:3 * W].rearrange("p t (k w) -> p t w k", k=3),
                                  AX.X, ALU.add).then_inc(head_ready, 1)

            def combine3(b):
                W = HD + 1
                dve.wait_ge(head_ready, b * HEADS + HEADS)
                dve.wait_ge(all_ready, b * T + T)
                plus = head_out[:, :, :, 0:W].rearrange("p h t w -> p t h w")
                minus = head_out[:, :, :, W:2 * W].rearrange("p h t w -> p t h w")
                a = all_out[:, :, :, :]
                dve.tensor_tensor(a, a, minus, ALU.subtract).then_inc(v_att, ch.one())
                dve.wait_ge(v_att, ch.value)
                dve.tensor_tensor(a, a, beta[:, :, :].unsqueeze(3).broadcast_to([P, T, HEADS, W]), ALU.mult).then_inc(v_att, ch.one())
                dve.wait_ge(v_att, ch.value)
                dve.tensor_tensor(a, a, plus, ALU.add).then_inc(v_att, ch.one())
                dve.wait_ge(v_att, ch.value)
                dve.reciprocal(recip[:, :, :], a[:, :, :, HD]).then_inc(combined_ready, 1)

            def mask_rows(nb, t):
                if t % 2 == 0:
                    dve.wait_ge(adj_loaded[t // 2], nb * 16 + 16)
                dve.tensor_scalar(nmask[:, t, :], adj_sb[:, t, :], 0.0, -1.0, ALU.not_equal, ALU.add)\
                    .then_inc(nmask_ready, 1)

            def next_moments(nb, f, own):
                dve.wait_ge(x_loaded, nb * 16 + 16)
                moments_of(xin, n_st, n_mv, f, v_next, own, n_moments)

            def next_shift(nb, f):
                shift_of(n_mv, n_rstd, n_shift, f, nb * 2, n_rstd_ready, n_shift_ready)

            def first_moments(b, f, own):
                dve.wait_ge(x1_ready, b * 2 + f + 1)
                moments_of(x1, st, mv, f, v_next, own, moments)

            def attention(b, has_next, has_far):
                nonlocal ch
                ch = Own()
                nxt = Own()
                parts = iter([(t, part) for t in range(1, HALF) for part in range(3)])
                sums = iter(range(T))

                def run_top(n):
                    for _ in range(n if has_next else 0):
                        t, part = next(parts)
                        top(b + 1, nxt, t, part)

                def run_sum():
                    if has_next:
                        reduce(b + 1, next(sums))

                spread_max(b, 0)
                distances(b, 0)
                scaled_values(b, 0, 0)
                dve.wait_ge(mask_t_ready, b * T + 2)
                positive_and_other(b, 0)
                split(b, 0, 0)
                run_top(1)
                split_last(b, 0, 0)
                dve.wait_ge(mask_t_ready, b * T + T)
                for j in range(2, T, 2):
                    positive_and_other(b, j)
                run_sum()
                for t in range(T):
                    if t in (0, 1):
                        run_top(1)
                    combine1(b, t)
                    if t == 3:
                        run_sum()
                        layer_moments(b, 1, 0)
                    if t == 5:
                        layer_shift(b, 1, 0)
                layer_moments(b, 1, 1)
                layer_shift(b, 1, 1)
                run_top(3)
                run_sum()
                for t in range(T + 2):
                    if t < T:
                        masked_max(b, t)
                    if t >= 2:
                        combine2(b, t - 2)
                    if t in (0, 1, 2):
                        run_top(1)
                    if t in (2, 7):
                        run_sum()
                    if has_far and t == 3:
                        for f in range(2):
                            next_moments(b + 2, f, nxt)
                    if has_far and t == 5:
                        for f in range(2):
                            next_shift(b + 2, f)
                    if t == 5:
                        layer_moments(b, 2, 0)
                    if t == 7:
                        layer_shift(b, 2, 0)
                layer_moments(b, 2, 1)
                layer_shift(b, 2, 1)
                if has_next:
                    for t in range(T):
                        mask_rows(b + 1, t)
                spread_max(b, 1)
                distances(b, 1)
                scaled_values(b, 1, 0)
                positive(b, 0, 0)
                split(b, 1, 0)
                positive(b, 0, 1)
                split_last(b, 1, 0)
                scaled_values(b, 1, 1)
                for j in range(2, T):
                    positive(b, 0, j)
                split(b, 1, 1)
                for j in range(0, 3):
                    positive(b, 1, j)
                split_last(b, 1, 1)
                run_sum()
                for head in range(HEADS):
                    for j in range(3 if head == 1 else 0, T if head else 0):
                        positive(b, head, j)
                        if head and j == SUM_AFTER:
                            sum_head(b, head - 1)
                    if head:
                        sum_all(b, head - 1)
                    if head in (1, 3):
                        run_sum()
                    if has_next and head - 1 in AGG_LINEAR:
                        f = AGG_LINEAR.index(head - 1)
                        next_finish(b + 1, f)
                        first_moments(b + 1, f, nxt)
                    if has_next and head in NORM_SHIFT:
                        layer_shift(b + 1, 0, NORM_SHIFT.index(head))
                    if has_far:
                        if head in PAIR_TOP:
                            top(b + 2, nxt, 0, PAIR_TOP.index(head))
                sum_head(b, HEADS - 1)
                sum_all(b, HEADS - 1)
                combine3(b)
                dve.wait_ge(v_att, ch.value)
                dve.sem_clear(v_att)
                if has_next:
                    dve.wait_ge(v_next, nxt.value)
                    dve.sem_clear(v_next)

            ch = None
            dve.wait_ge(consts, 7)
            nxt0 = Own()
            for f in range(2):
                next_moments(0, f, nxt0)
                next_shift(0, f)
            for part in range(3):
                top(0, nxt0, 0, part)
            dve.wait_ge(weights_in, N_WEIGHTS)
            sv = setup_v
            dve.tensor_copy(identb[:, :], ident[:, :]).then_inc(sv, 1)
            dve.tensor_scalar(ident_big[:, :], ident[:, :], MASKED, None, ALU.mult).then_inc(sv, 1)
            for k in range(2):
                dve.tensor_tensor(a3_prod, wcat[1][:, 0:C].rearrange("p (h f) -> p h f", h=HEADS),
                                  a3_sb[:, k * HD:(k + 1) * HD].unsqueeze(1).broadcast_to([P, HEADS, HD]),
                                  ALU.mult).then_inc(sv, 1)
                dve.wait_ge(sv, 3 + 2 * k)
                dve.tensor_reduce(wcat[1][:, C + k * HEADS:C + (k + 1) * HEADS], a3_prod, AX.X, ALU.add)\
                    .then_inc(sv, 1)
                dve.wait_ge(sv, 4 + 2 * k)
            dve.wait_ge(setup_pe, 1)
            dve.tensor_copy(wcat[0][:, C:C + 2], ps_e[:, 3, 0:2]).then_inc(sv, 1)
            dve.wait_ge(sv, 7)
            dve.tensor_copy(src_bc[:, 0, :], wcat[0][:, C:C + 1].broadcast_to([P, P]))
            dve.tensor_copy(src_bc[:, 1:1 + HEADS, :],
                            wcat[1][:, C:C + HEADS].unsqueeze(2).broadcast_to([P, HEADS, P])).then_inc(sv, 1)
            dve.wait_ge(setup_pe, 2)
            dve.tensor_copy(ww_turned, ps_e[:, 2, 0:C]).then_inc(sv, 1)
            dve.wait_ge(setup_pe, 3)
            dve.tensor_copy(qk_w[:, :, :].rearrange("p i c -> p (i c)"), ps_e[:, 1, 0:2 * C])
            dve.tensor_tensor(cols[:, 1:3], cols[:, 1:3], ps_e[:, 1, 2 * C:2 * C + 2], ALU.add).then_inc(sv, 1)
            dve.wait_ge(sv, 10)
            dve.tensor_scalar(cols[:, 3:4], cols[:, 1:2], SLOPE * SCORE_SCALE, None, ALU.mult).then_inc(sv, 1)

            for q in range(1, HALF):
                for part in range(3):
                    top(0, nxt0, q, part)
            for t in range(T):
                mask_rows(0, t)
            for f in range(2):
                next_moments(1, f, nxt0)
                next_shift(1, f)
            for t in range(4):
                reduce(0, t)
            for part in range(3):
                top(1, nxt0, 0, part)
            for t in range(4, T):
                reduce(0, t)
            for f in range(2):
                next_finish(0, f)
                first_moments(0, f, nxt0)
                layer_shift(0, 0, f)
            dve.wait_ge(v_next, nxt0.value)
            dve.sem_clear(v_next)
            with dve.Fori(0, B - 2) as b:
                attention(b, True, True)
            attention(B - 2, True, False)
            attention(B - 1, False, False)


_OUT = (8, 1024, 128)


def kernel(**inputs):
    import numpy as np
    import concourse.bacc as bacc
    from concourse import mybir as mb
    from concourse.bass_utils import run_bass_kernel_spmd

    def arr(name):
        return np.asarray(inputs[name])

    laid = {
        "x": arr("x"), "adj": arr("adj"), "w0": arr("L0_gnn_W"), "b0": arr("L0_gnn_b"),
        "w1": arr("L1_gnn_W"), "w1_t": arr("L1_gnn_W").T, "a1": arr("L1_gnn_a").reshape(2, 128).T,
        "ww_t": arr("L2_gnn_W_w").T, "wb": arr("L2_gnn_W_b"),
        "qw_t": arr("L2_gnn_Q_w").T, "qb": arr("L2_gnn_Q_b"),
        "kw_t": arr("L2_gnn_K_w").T, "kb": arr("L2_gnn_K_b"),
        "w3": arr("L3_gnn_W"), "a3": np.broadcast_to(arr("L3_gnn_a"), (128, 32)),
    }
    nc = bacc.Bacc("TRN2", target_bir_lowering=False, num_devices=1)
    arrays, args = {}, []
    for name, a in laid.items():
        a = np.ascontiguousarray(a)
        arrays[f"in_{name}"] = a
        args.append(nc.dram_tensor(f"in_{name}", a.shape, mb.dt.from_np(a.dtype), kind="ExternalInput").ap())
    args.append(nc.dram_tensor("out_x", _OUT, mb.dt.float32, kind="ExternalOutput").ap())
    graph_layers_kernel(nc, *args)
    r = run_bass_kernel_spmd(nc, [arrays], core_ids=[0])
    return r.results[0]["out_x"]
```
